# Optimizing a Trainium2 kernel written in Bass

```python
import numpy as np
import jax
import jax.numpy as jnp

def _softmax(x, axis=-1):
    return jax.nn.softmax(x, axis=axis)

def _gelu(x):
    return jax.nn.gelu(x, approximate=True)

def _silu(x):
    return jax.nn.silu(x)

def _sigmoid(x):
    return jax.nn.sigmoid(x)

def _layernorm(x, axis=-1, eps=1e-05):
    m = jnp.mean(x, axis=axis, keepdims=True)
    v = jnp.var(x, axis=axis, keepdims=True)
    return (x - m) / jnp.sqrt(v + eps)

def _scatter_add(tgt, idx, src, axis=0):
    return tgt.at[idx].add(src)

def _segment_sum(src, seg, n):
    return jax.ops.segment_sum(src, seg, n)
kernel_name = 'mk_perceiver_d1_seqx_r2_eb7e4a'

def setup_inputs(seed: int=0):
    np.random.seed(seed)
    _w = jnp.asarray

    def _rec_inputs():
        import jax
        import jax.numpy as jnp
        _rk = jax.random.key(seed)
        x = -0.0002928 + 1 * jax.random.normal(jax.random.fold_in(_rk, 1), (8, 64, 512), jnp.float32)
        _lenS = 64 - jax.random.randint(jax.random.fold_in(_rk, 7), (8,), 0, max(1, 64 // 4) + 1, jnp.int32)
        _lenS2 = 1601 - jax.random.randint(jax.random.fold_in(_rk, 8), (8,), 0, max(1, 1601 // 4) + 1, jnp.int32)
        _ctx_1024P = jax.random.normal(jax.random.fold_in(_rk, 11), (8, 16, 512), jnp.float32)
        _ctx_1024c = jax.random.dirichlet(jax.random.fold_in(_rk, 511), 0.3 * jnp.ones((16,), jnp.float32), (8, 1601))
        _ctx_1024t = jnp.einsum('bsk,bkd->bsd', _ctx_1024c, _ctx_1024P)
        _ctx_1024t = _ctx_1024t * jax.lax.rsqrt(jnp.mean(jnp.square(_ctx_1024t)) + 1e-12) * 0.953939
        ctx_1024 = -1.39393e-06 + 0.999914 * (_ctx_1024t + 0.3 * jax.random.normal(jax.random.fold_in(_rk, 611), (8, 1601, 512), jnp.float32))
        return (x, ctx_1024)
    x, ctx_1024 = _rec_inputs()

    def _L0_xattn_setup():
        import jax, jax.numpy as jnp
        import numpy as np
        EMBED_DIM = 512
        NUM_HEAD = 16
        HEAD_DIM = EMBED_DIM // NUM_HEAD
        SCALE = HEAD_DIM ** (-0.5)
        key = jax.random.key(seed)
        ks = jax.random.split(key, 8)
        B, N, K, D = (2, 1024, 1024, EMBED_DIM)
        s = D ** (-0.5)
        return {'x': jax.random.normal(ks[0], (B, N, D), jnp.float32), 'ctx': jax.random.normal(ks[1], (B, K, D), jnp.float32), 'Wq': jax.random.normal(ks[2], (D, D), jnp.float32) * s, 'bq': jnp.zeros((D,), jnp.float32), 'Wkv': jax.random.normal(ks[3], (D, 2 * D), jnp.float32) * s, 'bkv': jnp.zeros((2 * D,), jnp.float32), 'Wproj': jax.random.normal(ks[4], (D, D), jnp.float32) * s, 'bproj': jnp.zeros((D,), jnp.float32)}
    _L0_xattn_all = _L0_xattn_setup()
    _L0_xattn_in = {k: v for k, v in _L0_xattn_all.items() if k in ('Wq', 'bq', 'Wkv', 'bkv', 'Wproj', 'bproj')}
    del _L0_xattn_all

    def _L0_attn_setup():
        import jax, jax.numpy as jnp
        import numpy as np
        B, S, E = (4, 512, 512)
        N, D = (16, 64)
        key = jax.random.key(seed)
        k0, k1, k2, k3, k4 = jax.random.split(key, 5)
        return {'inputs': jax.random.normal(k0, (B, S, E), dtype=jnp.float32), 'WQ': jax.random.normal(k1, (N, E, D), dtype=jnp.float32) * 0.02, 'WK': jax.random.normal(k2, (N, E, D), dtype=jnp.float32) * 0.02, 'WV_down': jax.random.normal(k3, (N, E, D), dtype=jnp.float32) * 0.02, 'WV_up': jax.random.normal(k4, (N, D, E), dtype=jnp.float32) * 0.02}
    _L0_attn_all = _L0_attn_setup()
    _L0_attn_in = {k: v for k, v in _L0_attn_all.items() if k in ('WQ', 'WK', 'WV_down', 'WV_up')}
    del _L0_attn_all

    def _L0_ffn_setup():
        import jax, jax.numpy as jnp
        import numpy as np
        B, T, D, H, E, K = (2, 1024, 512, 2048, 8, 2)
        EPS = 1e-12

        def moe_forward(x, Wg, bg, W1, b1, W2, b2):
            gates = jax.nn.softmax(x @ Wg + bg, axis=-1)
            _, top_idx = jax.lax.top_k(gates, K)
            mask = jax.nn.one_hot(top_idx, E, dtype=gates.dtype).sum(axis=-2)
            g = gates * mask
            g = g / jnp.maximum(jnp.sum(jnp.abs(g), axis=-1, keepdims=True), EPS)
            h = jnp.einsum('btd,edh->bteh', x, W1) + b1[None, None]
            h = jax.nn.gelu(h, approximate=False)
            eo = jnp.einsum('bteh,ehd->bted', h, W2) + b2[None, None]
            return jnp.einsum('bte,bted->btd', g, eo)
        key = jax.random.key(seed)
        ks = jax.random.split(key, 8)
        s_d = 1.0 / np.sqrt(D)
        s_h = 1.0 / np.sqrt(H)
        return {'x': jax.random.normal(ks[0], (B, T, D), dtype=jnp.float32), 'Wg': jax.random.uniform(ks[1], (D, E), jnp.float32, -s_d, s_d), 'bg': jax.random.uniform(ks[2], (E,), jnp.float32, -s_d, s_d), 'W1': jax.random.uniform(ks[3], (E, D, H), jnp.float32, -s_d, s_d), 'b1': jax.random.uniform(ks[4], (E, H), jnp.float32, -s_d, s_d), 'W2': jax.random.uniform(ks[5], (E, H, D), jnp.float32, -s_h, s_h), 'b2': jax.random.uniform(ks[6], (E, D), jnp.float32, -s_h, s_h)}
    _L0_ffn_all = _L0_ffn_setup()
    _L0_ffn_in = {k: v for k, v in _L0_ffn_all.items() if k in ('Wg', 'bg', 'W1', 'b1', 'W2', 'b2')}
    del _L0_ffn_all
    return {'x': x, 'ctx_1024': ctx_1024, 'L0_xattn_Wq': _L0_xattn_in['Wq'], 'L0_xattn_bq': _L0_xattn_in['bq'], 'L0_xattn_Wkv': _L0_xattn_in['Wkv'], 'L0_xattn_bkv': _L0_xattn_in['bkv'], 'L0_xattn_Wproj': _L0_xattn_in['Wproj'], 'L0_xattn_bproj': _L0_xattn_in['bproj'], 'L0_attn_WQ': _L0_attn_in['WQ'], 'L0_attn_WK': _L0_attn_in['WK'], 'L0_attn_WV_down': _L0_attn_in['WV_down'], 'L0_attn_WV_up': _L0_attn_in['WV_up'], 'L0_ffn_Wg': _L0_ffn_in['Wg'], 'L0_ffn_bg': _L0_ffn_in['bg'], 'L0_ffn_W1': _L0_ffn_in['W1'], 'L0_ffn_b1': _L0_ffn_in['b1'], 'L0_ffn_W2': _L0_ffn_in['W2'], 'L0_ffn_b2': _L0_ffn_in['b2']}

def reference(x, ctx_1024, L0_xattn_Wq, L0_xattn_bq, L0_xattn_Wkv, L0_xattn_bkv, L0_xattn_Wproj, L0_xattn_bproj, L0_attn_WQ, L0_attn_WK, L0_attn_WV_down, L0_attn_WV_up, L0_ffn_Wg, L0_ffn_bg, L0_ffn_W1, L0_ffn_b1, L0_ffn_W2, L0_ffn_b2):
    import jax
    import jax.numpy as jnp

    def _L0_xattn_ref(x, ctx, Wq, bq, Wkv, bkv, Wproj, bproj):
        import jax, jax.numpy as jnp
        import numpy as np
        EMBED_DIM = 512
        NUM_HEAD = 16
        HEAD_DIM = EMBED_DIM // NUM_HEAD
        SCALE = HEAD_DIM ** (-0.5)
        B, N, D = x.shape
        K = ctx.shape[1]
        H, hd = (NUM_HEAD, HEAD_DIM)
        q = (x @ Wq + bq).reshape(B, N, H, hd).transpose(0, 2, 1, 3)
        kv = (ctx @ Wkv + bkv).reshape(B, K, 2, H, hd).transpose(2, 0, 3, 1, 4)
        k, v = (kv[0], kv[1])
        attn = jnp.einsum('bhnd,bhkd->bhnk', q * SCALE, k)
        attn = jax.nn.softmax(attn, axis=-1)
        out = jnp.einsum('bhnk,bhkd->bhnd', attn, v)
        out = out.transpose(0, 2, 1, 3).reshape(B, N, D)
        return out @ Wproj + bproj

    def _L0_attn_ref(inputs, WQ, WK, WV_down, WV_up):
        import jax, jax.numpy as jnp
        import numpy as np
        B, S, E = (4, 512, 512)
        N, D = (16, 64)
        d = WQ.shape[-1]
        Q = jnp.einsum('bse,ned->nbsd', inputs, WQ)
        K = jnp.einsum('bse,ned->nbsd', inputs, WK)
        scores = jnp.einsum('nbsd,nbSd->nbsS', K, Q) / jnp.sqrt(jnp.float32(d))
        scores = jnp.triu(scores)
        scores = jnp.where(scores == 0, jnp.finfo(jnp.float32).min, scores)
        attn = jax.nn.softmax(scores, axis=-1)
        inp_down = jnp.einsum('bse,ned->nbsd', inputs, WV_down)
        v_down = jnp.einsum('nbss,nbsd->nbsd', attn, inp_down)
        V = jnp.einsum('nbsd,nde->nbse', v_down, WV_up)
        delta_e = jnp.mean(V, axis=0)
        return inputs + delta_e

    def _L0_ffn_ref(x, Wg, bg, W1, b1, W2, b2):
        import jax, jax.numpy as jnp
        import numpy as np
        B, T, D, H, E, K = (2, 1024, 512, 2048, 8, 2)
        EPS = 1e-12

        def moe_forward(x, Wg, bg, W1, b1, W2, b2):
            gates = jax.nn.softmax(x @ Wg + bg, axis=-1)
            _, top_idx = jax.lax.top_k(gates, K)
            mask = jax.nn.one_hot(top_idx, E, dtype=gates.dtype).sum(axis=-2)
            g = gates * mask
            g = g / jnp.maximum(jnp.sum(jnp.abs(g), axis=-1, keepdims=True), EPS)
            h = jnp.einsum('btd,edh->bteh', x, W1) + b1[None, None]
            h = jax.nn.gelu(h, approximate=False)
            eo = jnp.einsum('bteh,ehd->bted', h, W2) + b2[None, None]
            return jnp.einsum('bte,bted->btd', g, eo)
        return moe_forward(x, Wg, bg, W1, b1, W2, b2)
    x = x + _L0_xattn_ref(_layernorm(x, axis=-1), ctx_1024, L0_xattn_Wq, L0_xattn_bq, L0_xattn_Wkv, L0_xattn_bkv, L0_xattn_Wproj, L0_xattn_bproj)
    x = x + _L0_attn_ref(_layernorm(x, axis=-1), L0_attn_WQ, L0_attn_WK, L0_attn_WV_down, L0_attn_WV_up)
    x = x + _L0_ffn_ref(_layernorm(x, axis=-1), L0_ffn_Wg, L0_ffn_bg, L0_ffn_W1, L0_ffn_b1, L0_ffn_W2, L0_ffn_b2)
    return x

_drawn_inputs = setup_inputs


def setup_inputs(seed=0):
    import zlib

    import numpy as np

    out = dict(_drawn_inputs(seed))
    spreads = {'L0_xattn_bq': (0.0, 0.406), 'L0_xattn_bkv': (0.0, 0.1), 'L0_xattn_bproj': (0.0, 0.1)}
    factors = {'L0_attn_WQ': 8.0,
     'L0_attn_WK': 8.0,
     'L0_attn_WV_down': 8.0,
     'L0_attn_WV_up': 8.0,
     'L0_ffn_bg': 4.436,
     'L0_ffn_b1': 8.0,
     'L0_ffn_b2': 8.0}
    for name, (base, spread) in spreads.items():
        noise = np.random.default_rng([zlib.crc32(name.encode()), seed]).standard_normal(out[name].shape)
        drawn = base * np.exp(spread * noise) if base else spread * noise
        out[name] = jnp.asarray(drawn.astype(out[name].dtype))
    for name, factor in factors.items():
        out[name] = (out[name] * factor).astype(out[name].dtype)
    return out
```

```python
from contextlib import ExitStack

import concourse.bass as bass
from concourse import mybir
from concourse.alu_op_type import AluOpType as ALU

ACT = mybir.ActivationFunctionType
F32 = mybir.dt.float32
FR = mybir.dt.float32r
BF16 = mybir.dt.bfloat16
I32 = mybir.dt.int32
AX = mybir.AxisListType



def f32(ap):
    return ap.bitcast(F32)


def perceiver_kernel(nc, x_in, ctx_in, Wq, bq, Wkv, bkv, Wproj, bproj,
                     WQ, WK, WVd, WVu, Wg, bg, W1, b1, W2, b2, out):
    B, S, D = x_in.shape
    CK = ctx_in.shape[1]
    P = 128
    T = B * S
    TT = T // P
    KC = D // P
    NH = 16
    HD = D // NH
    NP = NH // 2
    QK_SCALE = HD ** -0.5
    NT = -(-CK // P)
    TAIL = CK - (NT - 1) * P
    KEYS = CK + CK % 2
    GROUPS = [(2 * g, 2) for g in range(NT // 2)]
    GROUPS[-1] = (GROUPS[-1][0], NT - GROUPS[-1][0])
    NG = len(GROUPS)
    GMAX = KEYS - GROUPS[-1][0] * P
    assert NG % 2 == 0 and T == 512 and D == 512 and GMAX <= 512
    S0 = 2 * ((4 * 512 - KEYS) // 4)
    S_PARTS = [(max(0, 512 * c - S0), min(KEYS, 512 * (c + 1) - S0)) for c in range(4)]
    assert min(b - a for a, b in S_PARTS) >= 256
    S_HALVES = [(0, S_PARTS[1][1]), (S_PARTS[2][0], CK)]
    KV_USES = NG * KC + NT
    PT_GROUPS = -(-NT // 4)
    EPS = 1e-5

    x_rows = x_in.rearrange("b s d -> (b s) d").rearrange("(t p) d -> p t d", p=P)
    out_rows = out.rearrange("b s d -> (b s) d").rearrange("(t p) d -> p t d", p=P)

    q_dram = [nc.dram_tensor(f"qd_{part}", [D, T], F32, kind="Internal").ap() for part in ("hi", "lo")]
    r_dram = nc.dram_tensor("inverse_sums", [2, NP, T], F32, kind="Internal").ap()
    o_dram = nc.dram_tensor("o_heads", [NP, P, T], F32, kind="Internal").ap()

    with ExitStack() as whole:
        sems = {}

        def sem(name):
            if name not in sems:
                sems[name] = whole.enter_context(nc.semaphore(name))
            return sems[name]

        def sb(scope, name, shape, dt=F32):
            return scope.enter_context(nc.sbuf_tensor(name, shape, dt))

        def ps(name, shape):
            return whole.enter_context(nc.psum_tensor(name, shape, F32))

        psS = ps("ps_scores", [P, 4, 512])
        psS_row = psS[:, :, :].rearrange("p a c -> p (a c)")
        psT = [ps(f"ps_turn{i}", [P, 512]) for i in range(3)]
        psO = ps("ps_out", [P, 512])

        def bank(i):
            return psS[:, i, :] if i < 4 else (psT + [psO])[i - 4][:, :]

        ident = sb(whole, "ident", [P, P])
        ident_r = sb(whole, "ident_r", [P, P], FR)

        def norm_vector(dve, n, x, xn, tmp):
            done = sem(f"ln{n}_step")
            at = [0]

            def link(ins):
                at[0] += 1
                ins.then_inc(done, 1)
                dve.wait_ge(done, at[0])
            stats, mv, ve, root, rs = tmp
            for t in range(TT):
                ins = nc.vector.bn_stats(stats[:, t, :], x[:, t, :])
            link(ins)
            for t in range(TT):
                ins = nc.vector.bn_aggr(mv[:, t, :], stats[:, t, :])
            link(ins)
            nc.vector.tensor_scalar(ve[:, :], mv[:, :, 1], EPS, None, ALU.add).then_inc(sem(f"ln{n}_var"), 1)
            dve.wait_ge(sem(f"ln{n}_root"), 1)
            link(nc.vector.reciprocal(root[:, :], root[:, :]))
            link(nc.vector.tensor_tensor(rs[:, :], root[:, :], root[:, :], ALU.mult))
            link(nc.vector.tensor_tensor(rs[:, :], rs[:, :], ve[:, :], ALU.mult))
            link(nc.vector.tensor_scalar(rs[:, :], rs[:, :], -0.5, 1.5, ALU.mult, ALU.add))
            link(nc.vector.tensor_tensor(rs[:, :], rs[:, :], root[:, :], ALU.mult))
            for t in range(TT):
                ins = nc.vector.tensor_scalar(xn[:, t, :], x[:, t, :], mv[:, t, 0:1], rs[:, t:t + 1],
                                              ALU.subtract, ALU.mult)
            ins.then_inc(sem(f"ln{n}_done"), 1)

        def norm_scalar(act, n, tmp):
            act.wait_ge(sem(f"ln{n}_var"), 1)
            nc.scalar.activation(tmp[3][:, :], tmp[2][:, :], ACT.Sqrt).then_inc(sem(f"ln{n}_root"), 1)

        def turn_tensor(pe, n, xn):
            pe.wait_ge(sem(f"ln{n}_done"), 1)
            for k in range(KC):
                for t in range(TT):
                    ins = nc.tensor.matmul(bank(k)[:, t * P:(t + 1) * P], xn[:, t, k * P:(k + 1) * P],
                                           ident[:, :], is_transpose=True, start=True, stop=True)
                ins.then_inc(sem(f"turned{n}"), 1)

        def turn_scalar(act, n, hi):
            for k in range(KC):
                act.wait_ge(sem(f"turned{n}"), k + 1)
                nc.scalar.copy(hi[:, k, :], bank(k)).then_inc(sem(f"turned{n}_hi"), 1)

        def turn_vector(dve, n, hi, lo):
            for k in range(KC):
                dve.wait_ge(sem(f"turned{n}_hi"), k + 1)
                nc.vector.tensor_tensor(lo[:, k, :], bank(k), f32(hi[:, k, :]), ALU.subtract) \
                    .then_inc(sem(f"turned{n}_lo"), 1)

        def three(pe, out_ap, pairs):
            last = None
            for i, ((sh, sl), (mh, ml)) in enumerate(pairs):
                nc.tensor.matmul(out_ap, sh, mh, start=(i == 0), stop=False)
                nc.tensor.matmul(out_ap, sh, ml, start=False, stop=False)
                last = nc.tensor.matmul(out_ap, sl, mh, start=False, stop=(i == len(pairs) - 1))
            return last

        scope = ExitStack()
        Wkv_hi = sb(scope, "Wkv_hi", [P, KC, 2 * D], FR)
        Wkv_lo = sb(scope, "Wkv_lo", [P, KC, 2 * D], FR)
        bkc = sb(scope, "bkc", [64, NP])
        raw = sb(scope, "raw", [P, 2, 3, D])
        cT_hi = sb(scope, "cT_hi", [P, 2, KC, GMAX], FR)
        cT_lo = sb(scope, "cT_lo", [P, 2, KC, GMAX], FR)
        Qs_hi = sb(scope, "Qs_hi", [P, NP, P], FR)
        Qs_lo = sb(scope, "Qs_lo", [P, NP, P], FR)
        Pr = sb(scope, "Pr", [P, 2, CK])
        PT = sb(scope, "PT", [P, NT, 2, P], FR)
        U = sb(scope, "U", [P, NP, P])
        negmax = sb(scope, "negmax", [P, NP])
        halfmax = sb(scope, "halfmax", [P, NP, 2])
        half_sum = sb(scope, "half_sum", [P, NP, 2])
        total = sb(scope, "total", [P, NP, B])
        rinvT = sb(scope, "rinvT", [B * NP, P])
        prep = ExitStack()
        x_tok = sb(prep, "x_tok", [P, TT, D])
        xn = sb(prep, "xn", [P, TT, D])
        xT_hi = sb(prep, "xT_hi", [P, KC, T], FR)
        xT_lo = sb(prep, "xT_lo", [P, KC, T], FR)
        Wq_raw = sb(prep, "Wq_raw", [P, KC, D])
        Wq_hi = sb(prep, "Wq_hi", [P, KC, D], FR)
        Wq_lo = sb(prep, "Wq_lo", [P, KC, D], FR)
        bqc = sb(prep, "bqc", [P, KC])
        Wkv_raw = sb(prep, "Wkv_raw", [P, KC, 2 * D])
        q_sb = sb(prep, "q_sb", [P, KC, T])
        q_hi = sb(prep, "q_hi", [P, KC, T], FR)
        q_lo = sb(prep, "q_lo", [P, KC, T], FR)
        lnt1 = (sb(prep, "st1", [P, TT, 6]), sb(prep, "mv1", [P, TT, 2]), sb(prep, "ve1", [P, TT]),
                sb(prep, "rt1", [P, TT]), sb(prep, "rs1", [P, TT]))
        prep.close()
        Ks = sb(scope, "Ks", [P, NP, KEYS], FR)
        Vs = sb(scope, "Vs", [P, NT, NP, P], FR)
        scope.close()

        def uses_through(g):
            return sum(KC + n for _, n in GROUPS[:g + 1])

        def tile_rows(c):
            return TAIL if c == NT - 1 else P

        def group_cols(g):
            return (KEYS if g == NG - 1 else (GROUPS[g][0] + GROUPS[g][1]) * P) - GROUPS[g][0] * P

        with nc.Block() as block:

            def load_group(sp, b, g):
                c0, n = GROUPS[g]
                full = n if g < NG - 1 else n - 1
                src = ctx_in[bass.ds(b, 1), :, :].rearrange("a k d -> (a k) d")
                sp.dma_start(raw[:, g % 2, 0:full, :],
                             src[c0 * P:(c0 + full) * P, :].rearrange("(t p) d -> p t d", p=P)) \
                    .then_inc(sem(f"raw_in{g % 2}"), 16)
                if g == NG - 1:
                    sp.dma_start(raw[0:TAIL, g % 2, full, :], src[(c0 + full) * P:CK, :]) \
                        .then_inc(sem(f"raw_in{g % 2}"), 16)

            RAW_PER_BATCH = [16 * (NG // 2), 16 * (NG // 2 + 1)]

            def load_queries(sp, b):
                for part, dst in enumerate((Qs_hi, Qs_lo)):
                    src = q_dram[part].rearrange("(j h r) t -> h r j t", h=2, r=HD)
                    for h in range(2):
                        for twice in range(2):
                            r0 = 64 * twice + HD * h
                            sp.dma_start(f32(dst[r0:r0 + HD, :, S * h:S * (h + 1)]),
                                         src[h][:, :, bass.ds(b * S, S)]).then_inc(sem("q_in"), 16)

            def store_outputs(sp, b):
                for twice in range(2):
                    for h in range(2):
                        r0 = 64 * twice + HD * h
                        sp.dma_start(o_dram[:, r0:r0 + HD, bass.ds(b * S, S)].rearrange("j r t -> r j t"),
                                     U[r0:r0 + HD, :, S * h:S * (h + 1)]).then_inc(sem("u_free"), 16)

            @block.sync
            def _(sp):
                sp.dma_start(x_tok[:, :, :], x_rows).then_inc(sem("x_in"), 16)
                sp.dma_start(Wq_raw[:, :, :], Wq.rearrange("(k p) n -> p k n", p=P)).then_inc(sem("wq_in"), 16)
                sp.dma_start(bqc[:, :], bq.rearrange("(m p) -> p m", p=P), allow_slow_non_contiguous=True).then_inc(sem("bq_in"), 16)
                sp.dma_start(bkc[:, :], bkv[0:D].rearrange("(j r) -> r j", r=64), allow_slow_non_contiguous=True).then_inc(sem("bk_in"), 16)
                sp.dma_start(Wkv_raw[:, :, :], Wkv.rearrange("(k p) n -> p k n", p=P)).then_inc(sem("wkv_in"), 16)
                load_group(sp, 0, 0)
                load_group(sp, 0, 1)
                sp.wait_ge(sem("q_split"), 4)
                sp.dma_start(q_dram[0].rearrange("(m p) t -> p m t", p=P), f32(q_hi[:, :, :])).then_inc(sem("q_out"), 16)
                sp.dma_start(q_dram[1].rearrange("(m p) t -> p m t", p=P), f32(q_lo[:, :, :])).then_inc(sem("q_out"), 16)
                sp.wait_ge(sem("q_out"), 32)
                sp.wait_ge(sem("q_zeroed"), 2)
                load_queries(sp, 0)
                sp.sem_inc(sem("u_free"), 1)

                def loads_of_batch(b, last):
                    for g in range(NG):
                        if last and g + 2 >= NG:
                            break
                        sp.wait_ge(sem("c_turned"), b * (NG * KC) + KC * (g + 1))
                        load_group(sp, b + (g + 2) // NG, (g + 2) % NG)
                    if not last:
                        sp.wait_ge(sem("s_made"), (b + 1) * 2 * NP)
                        load_queries(sp, b + 1)
                    sp.wait_ge(sem("o_summed"), (b + 1) * NP)
                    store_outputs(sp, b)

                with sp.Fori(0, B - 1) as b:
                    loads_of_batch(b, False)
                loads_of_batch(B - 1, True)
                sp.wait_ge(sem("r_turned"), 1)
                sp.dma_start(r_dram.rearrange("h j (b t) -> (j b) h t", t=S), rinvT[:, :].rearrange("p (h t) -> p h t", h=2)) \
                    .then_inc(sem("r_out"), 16)
                sp.wait_ge(sem("r_out"), 16)
                sp.wait_ge(sem("u_free"), 64 * B + 1)

            @block.gpsimd
            def _(pool):
                nc.gpsimd.memset(ident[:, :], 0.0).then_inc(sem("ident0"), 1)
                pool.wait_ge(sem("ident0"), 1)
                nc.gpsimd.affine_select(out=ident[:, :], in_=ident[:, :], compare_op=ALU.not_equal, fill=1.0,
                                        base=0, pattern=[[-1, P]], channel_multiplier=1) \
                    .then_inc(sem("ident_ready"), 1)
                nc.gpsimd.memset(f32(Qs_hi[:, :, :]), 0.0).then_inc(sem("q_zeroed"), 1)
                nc.gpsimd.memset(f32(Qs_lo[:, :, :]), 0.0).then_inc(sem("q_zeroed"), 1)
                nc.gpsimd.memset(f32(cT_hi[:, :, :, GMAX - 1:GMAX]), 0.0).then_inc(sem("pad_zeroed"), 1)
                nc.gpsimd.memset(f32(cT_lo[:, :, :, GMAX - 1:GMAX]), 0.0).then_inc(sem("pad_zeroed"), 1)

            @block.scalar
            def _(act):
                norm_scalar(act, 1, lnt1)
                act.wait_ge(sem("wq_in"), 16)
                nc.scalar.copy(Wq_hi[:, :, :], Wq_raw[:, :, :]).then_inc(sem("wq_hi"), 1)
                turn_scalar(act, 1, xT_hi)
                act.wait_ge(sem("wkv_in"), 16)
                nc.scalar.copy(Wkv_hi[:, :, :], Wkv_raw[:, :, :]).then_inc(sem("wkv_hi"), 1)
                for m in range(KC):
                    act.wait_ge(sem("q_scaled"), m + 1)
                    nc.scalar.copy(q_hi[:, m, :], q_sb[:, m, :]).then_inc(sem("q_hi"), 1)
                act.wait_ge(sem("bk_in"), 16)

                with act.Fori(0, B) as b:
                    def turn_hi(g):
                        c0, n = GROUPS[g]
                        cols = CK - c0 * P if g == NG - 1 else n * P
                        if g >= 2:
                            act.wait_ge(sem("kv_made"), b * KV_USES + uses_through(g - 2))
                        for k in range(KC):
                            act.wait_ge(sem("c_turned"), b * (NG * KC) + g * KC + k + 1)
                            nc.scalar.copy(cT_hi[:, g % 2, k, 0:cols], psT[(g * KC + k) % 3][:, 0:cols]) \
                                .then_inc(sem("c_hi"), 1)

                    use = 0
                    turn_hi(0)
                    for g in range(NG):
                        if g + 1 < NG:
                            turn_hi(g + 1)
                        c0, n = GROUPS[g]
                        gc = group_cols(g)
                        for m in range(KC):
                            act.wait_ge(sem("kv_made"), b * KV_USES + use + 1)
                            for h in range(2):
                                j = 2 * m + h
                                ins = nc.scalar.activation(Ks[0:64, j, c0 * P:c0 * P + gc],
                                                           psS[64 * h:64 * h + 64, use % 4, 0:gc], ACT.Identity,
                                                           bias=bkc[:, j:j + 1])
                            ins.then_inc(sem("kv_hi"), 1)
                            use += 1
                        for c in range(c0, c0 + n):
                            act.wait_ge(sem("kv_made"), b * KV_USES + use + 1)
                            M = tile_rows(c)
                            nc.scalar.copy(Vs[0:M, c, :, 0:64],
                                           psS[0:M, use % 4, :].rearrange("p (j r) -> p j r", r=64)) \
                                .then_inc(sem("kv_hi"), 1)
                            use += 1

                    def turned_hi(j):
                        for q in range(PT_GROUPS):
                            act.wait_ge(sem("p_turned"), b * (NP * PT_GROUPS) + j * PT_GROUPS + q + 1)
                            if q == 0 and j >= 1:
                                act.wait_ge(sem("o_made"), b * NP + j)
                            n = min(4, NT - 4 * q)
                            M = P if n == 4 else TAIL
                            nc.scalar.copy(PT[0:M, 4 * q:4 * q + n, 0, :],
                                           psT[(j * PT_GROUPS + q) % 3][0:M, 0:n * P].rearrange("p (c r) -> p c r", r=P)) \
                                .then_inc(sem("pt_hi"), 1)

                    def exps(j):
                        act.wait_ge(sem("s_max"), b * NP + j + 1)
                        if j >= 2:
                            act.wait_ge(sem("p_turned"), b * (NP * PT_GROUPS) + (j - 1) * PT_GROUPS)
                        for half, (k0, k1) in enumerate(S_HALVES):
                            nc.scalar.activation(Pr[:, j % 2, k0:k1], psS_row[:, S0 + k0:S0 + k1], ACT.Exp,
                                                 bias=negmax[:, j:j + 1], accum_out=half_sum[:, j, half:half + 1]) \
                                .then_inc(sem("p_exp"), 1)

                    exps(0)
                    for j in range(NP):
                        if j + 1 < NP:
                            exps(j + 1)
                        turned_hi(j)
                act.wait_ge(sem("r_made"), 1)
                nc.scalar.copy(rinvT[:, :], bank(4)[0:B * NP, 0:P]).then_inc(sem("r_turned"), 1)

            @block.vector
            def _(dve):
                dve.wait_ge(sem("x_in"), 16)
                norm_vector(dve, 1, x_tok, xn, lnt1)
                dve.wait_ge(sem("wq_hi"), 1)
                nc.vector.tensor_tensor(Wq_lo[:, :, :], Wq_raw[:, :, :], f32(Wq_hi[:, :, :]), ALU.subtract) \
                    .then_inc(sem("wq_lo"), 1)
                turn_vector(dve, 1, xT_hi, xT_lo)
                dve.wait_ge(sem("bq_in"), 16)
                for m in range(KC):
                    dve.wait_ge(sem("q_made"), m + 1)
                    nc.vector.tensor_scalar(q_sb[:, m, :], bank(4 + m), bqc[:, m:m + 1], QK_SCALE,
                                            ALU.add, ALU.mult).then_inc(sem("q_scaled"), 1)
                for m in range(KC):
                    dve.wait_ge(sem("q_hi"), m + 1)
                    nc.vector.tensor_tensor(q_lo[:, m, :], q_sb[:, m, :], f32(q_hi[:, m, :]), ALU.subtract) \
                        .then_inc(sem("q_split"), 1)
                dve.wait_ge(sem("wkv_hi"), 1)
                nc.vector.tensor_tensor(Wkv_lo[:, :, :], Wkv_raw[:, :, :], f32(Wkv_hi[:, :, :]), ALU.subtract) \
                    .then_inc(sem("wkv_lo"), 1)
                dve.wait_ge(sem("q_out"), 32)
                dve.wait_ge(sem("bk_in"), 16)

                with dve.Fori(0, B) as b:
                    def turn_lo(g):
                        c0, n = GROUPS[g]
                        cols = CK - c0 * P if g == NG - 1 else n * P
                        for k in range(KC):
                            dve.wait_ge(sem("c_hi"), b * (NG * KC) + g * KC + k + 1)
                            nc.vector.tensor_tensor(cT_lo[:, g % 2, k, 0:cols], psT[(g * KC + k) % 3][:, 0:cols],
                                                    f32(cT_hi[:, g % 2, k, 0:cols]), ALU.subtract) \
                                .then_inc(sem("c_lo"), 1)

                    use = 0
                    turn_lo(0)
                    for g in range(NG):
                        if g + 1 < NG:
                            turn_lo(g + 1)
                        c0, n = GROUPS[g]
                        gc = group_cols(g)
                        for m in range(KC):
                            dve.wait_ge(sem("kv_hi"), b * KV_USES + use + 1)
                            for h in range(2):
                                j = 2 * m + h
                                cols = slice(c0 * P, c0 * P + gc)
                                ins = nc.vector.scalar_tensor_tensor(
                                    out=Ks[64:128, j, cols], in0=psS[64 * h:64 * h + 64, use % 4, 0:gc],
                                    scalar=bkc[:, j:j + 1], in1=f32(Ks[0:64, j, cols]),
                                    op0=ALU.add, op1=ALU.subtract)
                            ins.then_inc(sem("kv_lo"), 1)
                            use += 1
                        for c in range(c0, c0 + n):
                            dve.wait_ge(sem("kv_hi"), b * KV_USES + use + 1)
                            M = tile_rows(c)
                            nc.vector.tensor_tensor(Vs[0:M, c, :, 64:128],
                                                    psS[0:M, use % 4, :].rearrange("p (j r) -> p j r", r=64),
                                                    f32(Vs[0:M, c, :, 0:64]), ALU.subtract) \
                                .then_inc(sem("kv_lo"), 1)
                            use += 1

                    def row_max(j):
                        for half, (k0, k1) in enumerate(S_HALVES):
                            dve.wait_ge(sem("s_made"), (b * NP + j) * 2 + half + 1)
                            nc.vector.tensor_reduce(halfmax[:, j, half:half + 1], psS_row[:, S0 + k0:S0 + k1],
                                                    AX.X, ALU.max, negate=True).then_inc(sem("half_max"), 1)
                        dve.wait_ge(sem("half_max"), (b * NP + j) * 2 + 2)
                        nc.vector.tensor_reduce(negmax[:, j:j + 1], halfmax[:, j, :], AX.X, ALU.min) \
                            .then_inc(sem("s_max"), 1)

                    def turned_lo(j):
                        for q in range(PT_GROUPS):
                            dve.wait_ge(sem("pt_hi"), b * (NP * PT_GROUPS) + j * PT_GROUPS + q + 1)
                            n = min(4, NT - 4 * q)
                            M = P if n == 4 else TAIL
                            nc.vector.tensor_tensor(PT[0:M, 4 * q:4 * q + n, 1, :],
                                                    psT[(j * PT_GROUPS + q) % 3][0:M, 0:n * P].rearrange("p (c r) -> p c r", r=P),
                                                    f32(PT[0:M, 4 * q:4 * q + n, 0, :]), ALU.subtract) \
                                .then_inc(sem("pt_lo"), 1)

                    def out_sum(j):
                        dve.wait_ge(sem("o_made"), b * NP + j + 1)
                        if j == 0:
                            dve.wait_ge(sem("u_free"), b * 64 + 1)
                        nc.vector.tensor_reduce(U[:, j, :], psO[:, 0:2 * P].rearrange("p (a r) -> p r a", a=2),
                                                AX.X, ALU.add).then_inc(sem("o_summed"), 1)

                    row_max(0)
                    for j in range(NP):
                        if j + 1 < NP:
                            row_max(j + 1)
                        if j >= 1:
                            out_sum(j - 1)
                        turned_lo(j)
                    dve.wait_ge(sem("p_exp"), (b + 1) * 2 * NP)
                    nc.vector.tensor_tensor(total[:, :, bass.ds(b, 1)].rearrange("p j a -> p (j a)"),
                                            half_sum[:, :, 0], half_sum[:, :, 1], ALU.add).then_inc(sem("totals"), 1)
                    out_sum(NP - 1)
                dve.wait_ge(sem("totals"), B)
                nc.vector.reciprocal(total[:, :, :], total[:, :, :]).then_inc(sem("r_inverse"), 1)

            @block.tensor
            def _(pe):
                pe.wait_ge(sem("ident_ready"), 1)
                turn_tensor(pe, 1, xn)
                pe.wait_ge(sem("wq_lo"), 1)
                pe.wait_ge(sem("turned1_lo"), KC)
                for m in range(KC):
                    cols = slice(m * P, (m + 1) * P)
                    three(pe, bank(4 + m), [((Wq_hi[:, k, cols], Wq_lo[:, k, cols]), (xT_hi[:, k, :], xT_lo[:, k, :]))
                                            for k in range(KC)]).then_inc(sem("q_made"), 1)
                pe.wait_ge(sem("q_scaled"), KC)
                pe.wait_ge(sem("wkv_lo"), 1)
                pe.wait_ge(sem("pad_zeroed"), 2)

                with pe.Fori(0, B) as b:
                    def turn(g):
                        c0, n = GROUPS[g]
                        pe.wait_ge(sem(f"raw_in{g % 2}"),
                                   b * RAW_PER_BATCH[g % 2] + (16 * (g // 2 + 1) if g < NG - 1 else RAW_PER_BATCH[1]))
                        for k in range(KC):
                            if g * KC + k >= 3:
                                pe.wait_ge(sem("c_lo"), b * (NG * KC) + g * KC + k - 2)
                            for i in range(n):
                                M = tile_rows(c0 + i)
                                ins = nc.tensor.matmul(psT[(g * KC + k) % 3][:, i * P:i * P + M],
                                                       raw[0:M, g % 2, i, k * P:(k + 1) * P], ident[0:M, 0:M],
                                                       is_transpose=True, start=True, stop=True)
                            ins.then_inc(sem("c_turned"), 1)

                    use = 0
                    turn(0)
                    for g in range(NG):
                        if g + 1 < NG:
                            turn(g + 1)
                        c0, n = GROUPS[g]
                        gc = group_cols(g)
                        pe.wait_ge(sem("c_lo"), b * (NG * KC) + KC * (g + 1))
                        for m in range(KC):
                            if use >= 4:
                                pe.wait_ge(sem("kv_lo"), b * KV_USES + use - 3)
                            cols = slice(m * P, (m + 1) * P)
                            three(pe, psS[:, use % 4, 0:gc],
                                  [((Wkv_hi[:, k, cols], Wkv_lo[:, k, cols]),
                                    (cT_hi[:, g % 2, k, 0:gc], cT_lo[:, g % 2, k, 0:gc])) for k in range(KC)]) \
                                .then_inc(sem("kv_made"), 1)
                            use += 1
                        for c in range(c0, c0 + n):
                            pe.wait_ge(sem("kv_lo"), b * KV_USES + use - 3)
                            M = tile_rows(c)
                            rows = slice((c - c0) * P, (c - c0) * P + M)
                            ins = three(pe, psS[0:M, use % 4, :],
                                        [((cT_hi[:, g % 2, k, rows], cT_lo[:, g % 2, k, rows]),
                                          (Wkv_hi[:, k, D:2 * D], Wkv_lo[:, k, D:2 * D])) for k in range(KC)])
                            ins.then_inc(sem("kv_made"), 1)
                            use += 1

                    def scores(j):
                        for half in range(2):
                            if j >= 1:
                                pe.wait_ge(sem("p_exp"), (b * NP + j - 1) * 2 + half + 1)
                            for part, Q in enumerate((Qs_hi, Qs_lo)):
                                for k0, k1 in S_PARTS[2 * half:2 * half + 2]:
                                    ins = nc.tensor.matmul(psS_row[:, S0 + k0:S0 + k1], Q[:, j, :], Ks[:, j, k0:k1],
                                                           start=(part == 0), stop=(part == 1))
                            ins.then_inc(sem("s_made"), 1)

                    def turn_probs(j):
                        pe.wait_ge(sem("p_exp"), (b * NP + j + 1) * 2)
                        for q in range(PT_GROUPS):
                            n = j * PT_GROUPS + q
                            if n >= 3:
                                pe.wait_ge(sem("pt_lo"), b * (NP * PT_GROUPS) + n - 2)
                            for i in range(min(4, NT - 4 * q)):
                                c = 4 * q + i
                                M = tile_rows(c)
                                ins = nc.tensor.matmul(psT[n % 3][0:M, i * P:(i + 1) * P],
                                                       Pr[:, j % 2, c * P:c * P + M], ident[:, :],
                                                       is_transpose=True, start=True, stop=True)
                            ins.then_inc(sem("p_turned"), 1)

                    def outputs(j):
                        pe.wait_ge(sem("pt_lo"), b * (NP * PT_GROUPS) + (j + 1) * PT_GROUPS)
                        if j >= 1:
                            pe.wait_ge(sem("o_summed"), b * NP + j)
                        for c in range(NT):
                            M = tile_rows(c)
                            ins = nc.tensor.matmul(psO[:, 0:2 * P], Vs[0:M, c, j, :],
                                                   PT[0:M, c, :, :].rearrange("p a r -> p (a r)"),
                                                   start=(c == 0), stop=(c == NT - 1))
                        ins.then_inc(sem("o_made"), 1)

                    pe.wait_ge(sem("kv_lo"), (b + 1) * KV_USES)
                    pe.wait_ge(sem("q_in"), (b + 1) * 128)
                    scores(0)
                    for j in range(NP):
                        if j + 1 < NP:
                            scores(j + 1)
                        if j >= 1:
                            outputs(j - 1)
                        turn_probs(j)
                    outputs(NP - 1)
                pe.wait_ge(sem("r_inverse"), 1)
                nc.tensor.matmul(bank(4)[0:B * NP, 0:P], total[:, :, :].rearrange("p j b -> p (j b)"), ident[:, :],
                                 is_transpose=True, start=True, stop=True).then_inc(sem("r_made"), 1)

        SH, SD = WQ.shape[0], WQ.shape[2]
        HH = SH // 2
        HP = HH // 2
        FMIN = -3.4028234663852886e38
        SG = HH * TT

        late = whole.enter_context(ExitStack())
        x_sum = sb(late, "x_sum", [P, TT, D])
        scope = ExitStack()
        xn2 = sb(scope, "xn2", [P, TT, D])
        x2T_hi = sb(scope, "x2T_hi", [P, KC, T], FR)
        x2T_lo = sb(scope, "x2T_lo", [P, KC, T], FR)
        lnt2 = (sb(scope, "st2", [P, TT, 6]), sb(scope, "mv2", [P, TT, 2]), sb(scope, "ve2", [P, TT]),
                sb(scope, "rt2", [P, TT]), sb(scope, "rs2", [P, TT]))
        triu = sb(scope, "triu", [P, 2, SD])
        diag = sb(scope, "diag", [P, SD])
        proj = ExitStack()
        oT = sb(proj, "oT", [P, NP, T])
        oR = sb(proj, "oR", [P, NP, T])
        oT_hi = sb(proj, "oT_hi", [P, NP, T], FR)
        oT_lo = sb(proj, "oT_lo", [P, NP, T], FR)
        Wp_raw = sb(proj, "Wp_raw", [P, NP, D])
        Wp_hi = sb(proj, "Wp_hi", [P, NP, D], FR)
        Wp_lo = sb(proj, "Wp_lo", [P, NP, D], FR)
        bvc = sb(proj, "bvc", [P, NP])
        bpr = sb(proj, "bpr", [P, D])
        proj.close()
        W2_raw = sb(scope, "sW_raw", [P, 2, KC, HH * SD])
        W2_hi = sb(scope, "sW_hi", [P, 2, KC, HH * SD], FR)
        W2_lo = sb(scope, "sW_lo", [P, 2, KC, HH * SD], FR)
        QT_hi = sb(scope, "QT_hi", [P, HP, T], FR)
        QT_lo = sb(scope, "QT_lo", [P, HP, T], FR)
        KT_hi = sb(scope, "KT_hi", [P, HP, 2, T], FR)
        KT_lo = sb(scope, "KT_lo", [P, HP, 2, T], FR)
        SC = sb(scope, "SC", [P, SG, SD])
        SE = sb(scope, "SE", [P, SG, SD])
        smax = sb(scope, "smax", [P, SG])
        sdiag = sb(scope, "sdiag", [P, SG])
        ssum = sb(scope, "ssum", [P, SG])
        attn = sb(scope, "attn", [P, HH, TT])
        vd = sb(scope, "vd", [P, TT, HH * SD])
        vT_hi = sb(scope, "vT_hi", [P, HP, T], FR)
        vT_lo = sb(scope, "vT_lo", [P, HP, T], FR)
        scope.close()

        S_BANKS = HH * TT // 2
        USES = 2 * HP + S_BANKS + TT + HP
        HIS = 3 * HP

        with nc.Block() as block:

            @block.sync
            def _(sp):
                wp = Wproj.rearrange("(j r) n -> r j n", r=64)
                for twice in range(2):
                    for h in range(2):
                        r0 = 64 * twice + HD * h
                        sp.dma_start(oR[r0:r0 + HD, :, :], r_dram[h].partition_broadcast(HD)) \
                            .then_inc(sem("oR_in"), 16)
                for j0 in range(0, NP, 4):
                    sp.dma_start(oT[:, j0:j0 + 4, :], o_dram[j0:j0 + 4].rearrange("j p t -> p j t")) \
                        .then_inc(sem(f"oT_in{j0}"), 16)
                    for twice in range(2):
                        sp.dma_start(Wp_raw[64 * twice:64 * twice + 64, j0:j0 + 4, :], wp[:, j0:j0 + 4, :]) \
                            .then_inc(sem(f"wp_in{j0}"), 16)
                sp.dma_start(x_sum[:, :, :], x_rows).then_inc(sem("x_again"), 16)
                sp.dma_start(bpr[:, :], bproj.partition_broadcast(P)).then_inc(sem("bp_in"), 16)
                sp.wait_ge(sem("bv_zeroed"), 1)
                sp.dma_start(bvc[0:64, :], bkv[D:2 * D].rearrange("(j r) -> r j", r=64),
                             allow_slow_non_contiguous=True).then_inc(sem("bv_in"), 16)

                def load(w, src):
                    for k in range(KC):
                        sp.dma_start(W2_raw[:, w % 2, k, :], src(k)).then_inc(sem(f"sw_in{w % 2}"), 16)

                sp.wait_ge(sem("proj_made"), TT)
                for half in range(2):
                    heads = slice(HH * half, HH * half + HH)
                    for kind, W in enumerate((WQ, WK, WVd, WVu)):
                        w = 4 * half + kind
                        if w >= 2:
                            sp.wait_ge(sem("sw_lo"), w - 1)
                        if kind < 3:
                            for k in range(KC):
                                sp.dma_start(W2_raw[:, w % 2, k, :].rearrange("p (n d) -> p n d", d=SD),
                                             W[heads, k * P:(k + 1) * P, :].rearrange("n p d -> p n d")) \
                                    .then_inc(sem(f"sw_in{w % 2}"), 16)
                        else:
                            rows = W[heads].rearrange("n d e -> (n d) e")
                            for k in range(KC):
                                sp.dma_start(W2_raw[:, w % 2, k, :], rows[k * P:(k + 1) * P, :]) \
                                    .then_inc(sem(f"sw_in{w % 2}"), 16)

            @block.gpsimd
            def _(pool):
                nc.gpsimd.memset(bvc[:, :], 0.0).then_inc(sem("bv_zeroed"), 1)
                nc.gpsimd.memset(triu[:, :, :], 1.0).then_inc(sem("masks_set"), 1)
                nc.gpsimd.memset(diag[:, :], 0.0).then_inc(sem("masks_set"), 1)
                pool.wait_ge(sem("masks_set"), 2)
                for h in range(2):
                    rows = slice(64 * h, 64 * h + 64)
                    nc.gpsimd.affine_select(out=triu[rows, :, :], in_=triu[rows, :, :], compare_op=ALU.is_ge, fill=0.0,
                                            base=0, pattern=[[0, 2], [1, SD]], channel_multiplier=-1) \
                        .then_inc(sem("masks_ready"), 1)
                    nc.gpsimd.affine_select(out=diag[rows, :], in_=diag[rows, :], compare_op=ALU.not_equal, fill=1.0,
                                            base=0, pattern=[[1, SD]], channel_multiplier=-1) \
                        .then_inc(sem("masks_ready"), 1)
                pool.wait_ge(sem("proj_made"), TT)
                for h in range(2):
                    rows = slice(64 * h, 64 * h + 64)
                    nc.gpsimd.memset(f32(KT_hi[rows, :, 1 - h, :]), 0.0).then_inc(sem("kt_zeroed"), 1)
                    nc.gpsimd.memset(f32(KT_lo[rows, :, 1 - h, :]), 0.0).then_inc(sem("kt_zeroed"), 1)

            @block.scalar
            def _(act):
                for j0 in range(0, NP, 4):
                    act.wait_ge(sem(f"wp_in{j0}"), 32)
                    nc.scalar.copy(Wp_hi[:, j0:j0 + 4, :], Wp_raw[:, j0:j0 + 4, :]).then_inc(sem("wp_hi"), 1)
                for j in range(NP):
                    act.wait_ge(sem("bv_added"), j + 1)
                    nc.scalar.copy(oT_hi[:, j, :], oT[:, j, :]).then_inc(sem("oT_hi"), 1)
                norm_scalar(act, 2, lnt2)
                turn_scalar(act, 2, x2T_hi)

                def split_hi(w):
                    act.wait_ge(sem(f"sw_in{w % 2}"), 64 * (w // 2 + 1))
                    if w >= 2:
                        half, kind = (w - 2) // 4, (w - 2) % 4
                        if kind == 3:
                            act.wait_ge(sem("up_half"), 1)
                        else:
                            act.wait_ge(sem("b_made"), USES * half + (HP, 2 * HP, 2 * HP + S_BANKS + TT)[kind])
                    nc.scalar.copy(W2_hi[:, w % 2, :, :], W2_raw[:, w % 2, :, :]).then_inc(sem("sw_hi"), 1)

                act.wait_ge(sem("kt_zeroed"), 4)
                split_hi(0)
                split_hi(1)
                for half in range(2):
                    use = USES * half
                    for j in range(HP):
                        act.wait_ge(sem("b_made"), use + 1)
                        nc.scalar.copy(QT_hi[:, j, :], bank(4 + use % 4)).then_inc(sem("b_hi"), 1)
                        use += 1
                    split_hi(4 * half + 2)
                    for j in range(HP):
                        act.wait_ge(sem("b_made"), use + 1)
                        for h in range(2):
                            rows = slice(64 * h, 64 * h + 64)
                            ins = nc.scalar.copy(KT_hi[rows, j, h, :], bank(4 + use % 4)[rows, :])
                        ins.then_inc(sem("b_hi"), 1)
                        use += 1
                    split_hi(4 * half + 3)
                    act.wait_ge(sem("s_shifted"), half + 1)
                    nc.scalar.activation(SE[:, :, :], SE[:, :, :], ACT.Exp).then_inc(sem("s_exp"), 1)
                    nc.scalar.activation(sdiag[:, :], sdiag[:, :], ACT.Exp).then_inc(sem("s_exp"), 1)
                    if half == 0:
                        split_hi(4)
                    use = USES * half + 2 * HP + S_BANKS + TT
                    for j in range(HP):
                        act.wait_ge(sem("b_made"), use + 1)
                        nc.scalar.copy(vT_hi[:, j, :], bank(4 + use % 4)).then_inc(sem("b_hi"), 1)
                        use += 1
                    if half == 0:
                        split_hi(5)

            @block.vector
            def _(dve):
                dve.wait_ge(sem("oR_in"), 64)
                for j in range(NP):
                    if j % 4 == 0:
                        dve.wait_ge(sem(f"oT_in{j}"), 16)
                    nc.vector.tensor_tensor(oT[:, j, :], oT[:, j, :], oR[:, j, :], ALU.mult).then_inc(sem("o_normed"), 1)
                dve.wait_ge(sem("bv_in"), 16)
                for j in range(NP):
                    dve.wait_ge(sem("o_normed"), j + 1)
                    nc.vector.tensor_scalar(oT[:, j, :], oT[:, j, :], bvc[:, j:j + 1], None, ALU.add) \
                        .then_inc(sem("bv_added"), 1)
                for j0 in range(0, NP, 4):
                    dve.wait_ge(sem("wp_hi"), j0 // 4 + 1)
                    nc.vector.tensor_tensor(Wp_lo[:, j0:j0 + 4, :], Wp_raw[:, j0:j0 + 4, :],
                                            f32(Wp_hi[:, j0:j0 + 4, :]), ALU.subtract).then_inc(sem("wp_lo"), 1)
                    for j in range(j0, j0 + 4):
                        dve.wait_ge(sem("oT_hi"), j + 1)
                        nc.vector.tensor_tensor(oT_lo[:, j, :], oT[:, j, :], f32(oT_hi[:, j, :]), ALU.subtract) \
                            .then_inc(sem("oT_lo"), 1)
                dve.wait_ge(sem("x_again"), 16)
                dve.wait_ge(sem("bp_in"), 16)
                nc.vector.tensor_tensor(x_sum[:, :, :], x_sum[:, :, :],
                                        bpr[:, :].unsqueeze(1).broadcast_to([P, TT, D]), ALU.add) \
                    .then_inc(sem("x_base"), 1)
                dve.wait_ge(sem("x_base"), 1)
                for t in range(TT):
                    dve.wait_ge(sem("proj_made"), t + 1)
                    nc.vector.tensor_tensor(x_sum[:, t, :], x_sum[:, t, :], bank(t), ALU.add).then_inc(sem("x_1"), 1)
                dve.wait_ge(sem("x_1"), TT)
                norm_vector(dve, 2, x_sum, xn2, lnt2)
                turn_vector(dve, 2, x2T_hi, x2T_lo)
                dve.wait_ge(sem("ln2_done"), 1)
                nc.vector.tensor_tensor(x_sum[:, :, :], x_sum[:, :, :], xn2[:, :, :], ALU.add) \
                    .then_inc(sem("x_1"), 1)

                def split_lo(w):
                    dve.wait_ge(sem("sw_hi"), w + 1)
                    nc.vector.tensor_tensor(W2_lo[:, w % 2, :, :], W2_raw[:, w % 2, :, :],
                                            f32(W2_hi[:, w % 2, :, :]), ALU.subtract).then_inc(sem("sw_lo"), 1)

                step = [0]

                def link(ins):
                    step[0] += 1
                    ins.then_inc(sem("soft_step"), 1)
                    dve.wait_ge(sem("soft_step"), step[0])

                split_lo(0)
                split_lo(1)
                dve.wait_ge(sem("masks_ready"), 4)
                for half in range(2):
                    use, his = USES * half, HIS * half
                    for j in range(HP):
                        dve.wait_ge(sem("b_hi"), his + 1)
                        nc.vector.tensor_tensor(QT_lo[:, j, :], bank(4 + use % 4), f32(QT_hi[:, j, :]), ALU.subtract) \
                            .then_inc(sem("b_done"), 1)
                        use += 1
                        his += 1
                    split_lo(4 * half + 2)
                    for j in range(HP):
                        dve.wait_ge(sem("b_hi"), his + 1)
                        for h in range(2):
                            rows = slice(64 * h, 64 * h + 64)
                            ins = nc.vector.tensor_tensor(KT_lo[rows, j, h, :], bank(4 + use % 4)[rows, :],
                                                          f32(KT_hi[rows, j, h, :]), ALU.subtract)
                        ins.then_inc(sem("b_done"), 1)
                        use += 1
                        his += 1
                    split_lo(4 * half + 3)
                    for n in range(HH):
                        for w in range(TT // 2):
                            dve.wait_ge(sem("b_made"), use + 1)
                            blocks = bank(4 + use % 4).rearrange("p (a c) -> p a c", c=2 * SD)
                            for h in range(2):
                                rows = slice(64 * h, 64 * h + 64)
                                g0 = n * TT + 2 * w
                                ins = nc.vector.scalar_tensor_tensor(
                                    out=SC[rows, g0:g0 + 2, :], in0=blocks[rows, 0:4:3, 64 * h:64 * h + 64],
                                    scalar=SD ** -0.5, in1=triu[rows, :, :], op0=ALU.mult, op1=ALU.mult)
                            ins.then_inc(sem("b_done"), 1)
                            use += 1
                    dve.wait_ge(sem("b_done"), use)
                    link(nc.vector.tensor_scalar(SE[:, :, :], SC[:, :, :], 0.0, FMIN, ALU.is_equal, ALU.mult))
                    link(nc.vector.tensor_tensor(SC[:, :, :], SC[:, :, :], SE[:, :, :], ALU.add))
                    link(nc.vector.tensor_tensor(SE[:, :, :], SC[:, :, :],
                                                 diag[:, :].unsqueeze(1).broadcast_to([P, SG, SD]), ALU.mult))
                    link(nc.vector.tensor_reduce(sdiag[:, :], SE[:, :, :], AX.X, ALU.add))
                    link(nc.vector.tensor_reduce(smax[:, :], SC[:, :, :], AX.X, ALU.max))
                    link(nc.vector.tensor_tensor(sdiag[:, :], sdiag[:, :], smax[:, :], ALU.subtract))
                    nc.vector.tensor_tensor(SE[:, :, :], SC[:, :, :],
                                            smax[:, :].unsqueeze(2).broadcast_to([P, SG, SD]), ALU.subtract) \
                        .then_inc(sem("s_shifted"), 1)
                    dve.wait_ge(sem("s_exp"), 2 * half + 2)
                    link(nc.vector.tensor_reduce(ssum[:, :], SE[:, :, :], AX.X, ALU.add))
                    link(nc.vector.reciprocal(ssum[:, :], ssum[:, :]))
                    link(nc.vector.scalar_tensor_tensor(out=attn[:, :, :].rearrange("p n t -> p (n t)"),
                                                        in0=sdiag[:, :], scalar=1.0 / SH, in1=ssum[:, :],
                                                        op0=ALU.mult, op1=ALU.mult))
                    for t in range(TT):
                        dve.wait_ge(sem("b_made"), use + 1)
                        nc.vector.tensor_tensor(vd[:, t, :].rearrange("p (n d) -> p n d", d=SD),
                                                bank(4 + use % 4).rearrange("p (n d) -> p n d", d=SD),
                                                attn[:, :, t:t + 1].broadcast_to([P, HH, SD]), ALU.mult) \
                            .then_inc(sem("b_done"), 1)
                        use += 1
                    if half == 0:
                        split_lo(4)
                    for j in range(HP):
                        dve.wait_ge(sem("b_hi"), his + 1)
                        nc.vector.tensor_tensor(vT_lo[:, j, :], bank(4 + use % 4), f32(vT_hi[:, j, :]), ALU.subtract) \
                            .then_inc(sem("b_done"), 1)
                        use += 1
                        his += 1
                    if half == 0:
                        split_lo(5)
                dve.wait_ge(sem("x_1"), TT + 1)
                for t in range(TT):
                    dve.wait_ge(sem("up_made"), t + 1)
                    nc.vector.tensor_tensor(x_sum[:, t, :], x_sum[:, t, :], bank(t), ALU.add).then_inc(sem("x_2"), 1)

            @block.tensor
            def _(pe):
                for t in range(TT):
                    cols = slice(t * P, (t + 1) * P)
                    for j in range(NP):
                        if t == 0:
                            pe.wait_ge(sem("wp_lo"), j // 4 + 1)
                            pe.wait_ge(sem("oT_lo"), j + 1)
                        nc.tensor.matmul(bank(t), oT_hi[:, j, cols], Wp_hi[:, j, :], start=(j == 0), stop=False)
                        nc.tensor.matmul(bank(t), oT_hi[:, j, cols], Wp_lo[:, j, :], start=False, stop=False)
                        ins = nc.tensor.matmul(bank(t), oT_lo[:, j, cols], Wp_hi[:, j, :], start=False,
                                               stop=(j == NP - 1))
                    ins.then_inc(sem("proj_made"), 1)
                turn_tensor(pe, 2, xn2)
                pe.wait_ge(sem("turned2_lo"), KC)

                def take(use):
                    if use >= 4:
                        pe.wait_ge(sem("b_done"), use - 3)
                    return bank(4 + use % 4)

                for half in range(2):
                    use = USES * half

                    def columns(w):
                        nonlocal use
                        pe.wait_ge(sem("sw_lo"), w + 1)
                        for j in range(HP):
                            cols = slice(j * P, (j + 1) * P)
                            ins = three(pe, take(use), [((W2_hi[:, w % 2, k, cols], W2_lo[:, w % 2, k, cols]),
                                                         (x2T_hi[:, k, :], x2T_lo[:, k, :])) for k in range(KC)])
                            ins.then_inc(sem("b_made"), 1)
                            use += 1
                        return ins

                    columns(4 * half)
                    columns(4 * half + 1)
                    pe.wait_ge(sem("b_done"), use)
                    for n in range(HH):
                        j, h = n // 2, n % 2
                        for w in range(TT // 2):
                            out_bank = take(use)
                            for r in range(2):
                                g = 2 * w + r
                                keys = slice(g * P, (g + 1) * P)
                                window = slice(2 * w * P, 2 * (w + 1) * P)
                                ins = three(pe, out_bank[:, 2 * P * r:2 * P * (r + 1)],
                                            [((KT_hi[:, j, h, keys], KT_lo[:, j, h, keys]),
                                              (QT_hi[:, j, window], QT_lo[:, j, window]))])
                            ins.then_inc(sem("b_made"), 1)
                            use += 1
                    w = 4 * half + 2
                    pe.wait_ge(sem("sw_lo"), w + 1)
                    for t in range(TT):
                        cols = slice(t * P, (t + 1) * P)
                        three(pe, take(use), [((x2T_hi[:, k, cols], x2T_lo[:, k, cols]),
                                               (W2_hi[:, w % 2, k, :], W2_lo[:, w % 2, k, :])) for k in range(KC)]) \
                            .then_inc(sem("b_made"), 1)
                        use += 1
                    pe.wait_ge(sem("b_done"), use)
                    for j in range(HP):
                        b_out = take(use)
                        for t in range(TT):
                            ins = nc.tensor.matmul(b_out[:, t * P:(t + 1) * P], vd[:, t, j * P:(j + 1) * P],
                                                   ident[:, :], is_transpose=True, start=True, stop=True)
                        ins.then_inc(sem("b_made"), 1)
                        use += 1
                    w = 4 * half + 3
                    pe.wait_ge(sem("sw_lo"), w + 1)
                    pe.wait_ge(sem("b_done"), use)
                    for t in range(TT):
                        cols = slice(t * P, (t + 1) * P)
                        for j in range(HP):
                            first, last = half == 0 and j == 0, half == 1 and j == HP - 1
                            nc.tensor.matmul(bank(t), vT_hi[:, j, cols], W2_hi[:, w % 2, j, :], start=first, stop=False)
                            nc.tensor.matmul(bank(t), vT_hi[:, j, cols], W2_lo[:, w % 2, j, :], start=False, stop=False)
                            ins = nc.tensor.matmul(bank(t), vT_lo[:, j, cols], W2_hi[:, w % 2, j, :],
                                                   start=False, stop=last)
                        if half == 1:
                            ins.then_inc(sem("up_made"), 1)
                        elif t == TT - 1:
                            ins.then_inc(sem("up_half"), 1)

        NE, _, H = W1.shape
        TOP = 2
        SLOTS = 256
        SLT = SLOTS // P
        HC = H // P
        QT = HC // 4
        ITEMS = NE + (TOP * T) // (SLOTS + 1)
        assert T <= 2 * SLOTS
        FAR = 10000.0
        GATE_EPS = 1e-12
        UNITS = 2 * QT
        UNIT_ORDER = [("1", 0), ("1", 1), ("2", 0), ("1", 2), ("2", 1), ("1", 3), ("2", 2), ("2", 3)]
        UNIT_OF = {u: n for n, u in enumerate(UNIT_ORDER)}
        assert len(UNIT_ORDER) == UNITS and QT == 4

        scope = ExitStack()
        wu_raw = sb(scope, "wu_raw", [P, 4, 4, D])
        wu_hi = sb(scope, "wu_hi", [P, 4, 4, D], FR)
        wu_lo = sb(scope, "wu_lo", [P, 4, 4, D], FR)
        xn3 = sb(scope, "xn3", [P, TT, D])
        xg_hi = sb(scope, "xg_hi", [P, TT, D], FR)
        xg_lo = sb(scope, "xg_lo", [P, TT, D], FR)
        iota_s = sb(scope, "iota_s", [P, SLOTS])
        b1T = sb(scope, "b1T", [P, NE, HC])
        table = sb(scope, "table", [P, ITEMS, 2, TT])
        eid = sb(scope, "eid", [P, ITEMS], I32)
        n_items = sb(scope, "n_items", [P, 1], I32)
        cur = sb(scope, "cur", [P, 2, TT])
        b1c = sb(scope, "b1c", [P, HC])
        gate2 = sb(scope, "gate2", [P, TT, 2], FR)
        gating = ExitStack()
        lnt3 = (sb(gating, "st3", [P, TT, 6]), sb(gating, "mv3", [P, TT, 2]), sb(gating, "ve3", [P, TT]),
                sb(gating, "rt3", [P, TT]), sb(gating, "rs3", [P, TT]))
        x3T_hi = sb(gating, "x3T_hi", [P, KC, T], FR)
        x3T_lo = sb(gating, "x3T_lo", [P, KC, T], FR)
        Wg_raw = sb(gating, "Wg_raw", [P, KC, NE])
        Wg_hi = sb(gating, "Wg_hi", [P, KC, NE], FR)
        Wg_lo = sb(gating, "Wg_lo", [P, KC, NE], FR)
        bgr = sb(gating, "bgr", [P, NE])
        b1_raw = sb(gating, "b1_raw", [P, P])
        b2_sb = sb(gating, "b2_sb", [NE, D])
        gT = sb(gating, "gT", [NE, T])
        before = sb(gating, "before", [P, P], BF16)
        ones = sb(gating, "ones", [P, P], BF16)
        iota_e = sb(gating, "iota_e", [P, NE])
        rev_e = sb(gating, "rev_e", [P, TT, NE])
        iota_i = sb(gating, "iota_i", [P, ITEMS, NE])
        G3 = [P, TT, NE]
        gate = sb(gating, "gate", G3)
        work = sb(gating, "work", G3)
        key = sb(gating, "key", G3)
        hot1 = sb(gating, "hot1", G3)
        hot2 = sb(gating, "hot2", G3)
        rank = sb(gating, "rank", G3)
        chosen = sb(gating, "chosen", G3, BF16)
        col = sb(gating, "col", [P, TT])
        cnt = sb(gating, "cnt", [P, NE])
        start_at = sb(gating, "start_at", [P, NE + 1])
        I3 = [P, ITEMS, NE]
        in_e = sb(gating, "in_e", I3)
        tmp_i = sb(gating, "tmp_i", I3)
        base = sb(gating, "base", [P, ITEMS])
        gating.close()
        sel = sb(scope, "sel", [P, TT, SLOTS], FR)
        selT = sb(scope, "selT", [P, SLT, T], FR)
        gT_hi = sb(scope, "gT_hi", [P, KC, SLOTS], FR)
        gT_lo = sb(scope, "gT_lo", [P, KC, SLOTS], FR)
        gs = sb(scope, "gs", [P, SLT])
        hid = sb(scope, "hid", [P, 2, SLOTS])
        h_hi = sb(scope, "h_hi", [P, 2, 4, SLOTS], FR)
        h_lo = sb(scope, "h_lo", [P, 2, 4, SLOTS], FR)
        eo = sb(scope, "eo", [P, SLT, D])
        eo_hi = sb(scope, "eo_hi", [P, SLT, D], FR)
        eo_lo = sb(scope, "eo_lo", [P, SLT, D], FR)
        scope.close()

        L1_CREDIT, L2_CREDIT, WLO_CREDIT = HC, QT, 4

        def items_of(eng):
            return eng.value_load(n_items[0:1, 0:1], min_val=NE, max_val=ITEMS)

        with nc.Block() as block:

            @block.sync
            def _(sp):
                sp.dma_start(Wg_raw[:, :, :], Wg.rearrange("(k p) e -> p k e", p=P)).then_inc(sem("wg_in"), 16)
                sp.dma_start(bgr[:, :], bg.partition_broadcast(P)).then_inc(sem("bg_in"), 16)
                sp.dma_start(b1_raw[:, :], b1.rearrange("e (c p) -> (e c) p", p=P)).then_inc(sem("b1_in"), 16)
                sp.dma_start(b2_sb[:, :], b2).then_inc(sem("b2_in"), 16)
                sp.wait_ge(sem("table_ready"), 1)
                items = items_of(sp)
                with sp.Fori(0, items) as i:
                    e = sp.value_load(eid[0:1, bass.ds(i, 1)], min_val=0, max_val=NE - 1)
                    for v, (which, q) in enumerate(UNIT_ORDER):
                        sp.wait_ge(sem("wu_lo_done"), i * UNITS + v + 1)
                        W = (W1 if which == "1" else W2)[bass.ds(e, 1)].rearrange("a r c -> (a r) c")
                        if which == "1":
                            src = W[:, q * 4 * P:(q + 1) * 4 * P]
                        else:
                            src = W[q * 4 * P:(q + 1) * 4 * P, :]
                        sp.dma_start(wu_raw[:, v % 4, :, :], src.rearrange("(k p) c -> p k c", p=P)) \
                            .then_inc(sem(f"wu_in{v % 4}"), 16)
                for t in range(TT):
                    sp.wait_ge(sem("x_3"), t + 1)
                    sp.dma_start(out_rows[:, t, :], x_sum[:, t, :]).then_inc(sem("stored"), 16)
                sp.wait_ge(sem("stored"), 16 * TT)

            @block.gpsimd
            def _(pool):
                nc.gpsimd.memset(before[:, :], 1.0).then_inc(sem("c_set"), 1)
                nc.gpsimd.memset(ones[:, :], 1.0).then_inc(sem("c_set"), 1)
                pool.wait_ge(sem("c_set"), 2)
                nc.gpsimd.affine_select(out=before[:, :], in_=before[:, :], compare_op=ALU.is_gt, fill=0.0, base=0,
                                        pattern=[[1, P]], channel_multiplier=-1).then_inc(sem("c_ready"), 1)
                for t, pattern, at in ((iota_s, [[1, SLOTS]], 0), (iota_e, [[1, NE]], 0),
                                       (rev_e, [[0, TT], [-1, NE]], NE), (iota_i, [[1, ITEMS], [0, NE]], 0)):
                    nc.gpsimd.iota(t[tuple(slice(None) for _ in t.shape)], pattern, base=at, channel_multiplier=0,
                                   allow_small_or_imprecise_dtypes=True).then_inc(sem("c_ready"), 1)

            @block.scalar
            def _(act):
                norm_scalar(act, 3, lnt3)
                act.wait_ge(sem("ln3_done"), 1)
                nc.scalar.copy(xg_hi[:, :, :], xn3[:, :, :]).then_inc(sem("xg_hi"), 1)
                act.wait_ge(sem("wg_in"), 16)
                nc.scalar.copy(Wg_hi[:, :, :], Wg_raw[:, :, :]).then_inc(sem("wg_hi"), 1)
                nc.scalar.copy(ident_r[:, :], ident[:, :]).then_inc(sem("ident_r"), 1)
                turn_scalar(act, 3, x3T_hi)
                act.wait_ge(sem("g_shifted"), 1)
                nc.scalar.activation(gate[:, :, :], gate[:, :, :], ACT.Exp).then_inc(sem("g_exp"), 1)

                act.wait_ge(sem("table_ready"), 1)
                items = items_of(act)
                with act.Fori(0, items) as i:
                    def unit_hi(v):
                        act.wait_ge(sem(f"wu_in{v % 4}"), i * 32 + 16 * (v // 4 + 1))
                        which, q = UNIT_ORDER[v - 4]
                        back = 1 if v < 4 else 0
                        if which == "1":
                            act.wait_ge(sem("l1_made"), L1_CREDIT - back * HC + i * HC + 4 * (q + 1))
                        else:
                            act.wait_ge(sem("l2_made"), L2_CREDIT - back * QT + i * QT + q + 1)
                        nc.scalar.copy(wu_hi[:, v % 4, :, :], wu_raw[:, v % 4, :, :]).then_inc(sem("wu_hi_done"), 1)

                    def gelus(q):
                        for n in range(4 * q, 4 * q + 4):
                            act.wait_ge(sem("l1_made"), L1_CREDIT + i * HC + n + 1)
                            if n == 0:
                                act.wait_ge(sem("b1_ready"), i + 1)
                            if n >= 2:
                                act.wait_ge(sem("h_split"), i * HC + n - 1)
                            nc.scalar.activation(hid[:, n % 2, :], psT[n % 2][:, 0:SLOTS], ACT.Gelu,
                                                 bias=b1c[:, n:n + 1]).then_inc(sem("h_made"), 1)

                    unit_hi(0)
                    unit_hi(1)
                    for kk in range(2):
                        act.wait_ge(sem("g_made"), 2 * i + kk + 1)
                        nc.scalar.copy(gT_hi[:, 2 * kk:2 * kk + 2, :],
                                       psT[kk][:, :].rearrange("p (k s) -> p k s", s=SLOTS)).then_inc(sem("g_hi"), 1)
                    unit_hi(2)
                    for st in range(SLT):
                        act.wait_ge(sem("selT_made"), i * SLT + st + 1)
                        nc.scalar.copy(selT[:, st, :], bank(6 + st)).then_inc(sem("selT_done"), 1)
                    unit_hi(3)
                    gelus(0)
                    unit_hi(4)
                    gelus(1)
                    unit_hi(5)
                    gelus(2)
                    unit_hi(6)
                    gelus(3)
                    unit_hi(7)
                    act.wait_ge(sem("l2_made"), L2_CREDIT + (i + 1) * QT)
                    act.wait_ge(sem("gs_done"), i + 1)
                    for st in range(SLT):
                        nc.scalar.activation(eo[:, st, :], bank(6 + st), ACT.Copy, scale=gs[:, st:st + 1]) \
                            .then_inc(sem("eo_made"), 1)

            @block.vector
            def _(dve):
                norm_vector(dve, 3, x_sum, xn3, lnt3)
                dve.wait_ge(sem("xg_hi"), 1)
                nc.vector.tensor_tensor(xg_lo[:, :, :], xn3[:, :, :], f32(xg_hi[:, :, :]), ALU.subtract) \
                    .then_inc(sem("xg_lo"), 1)
                dve.wait_ge(sem("wg_hi"), 1)
                nc.vector.tensor_tensor(Wg_lo[:, :, :], Wg_raw[:, :, :], f32(Wg_hi[:, :, :]), ALU.subtract) \
                    .then_inc(sem("wg_lo"), 1)
                turn_vector(dve, 3, x3T_hi, x3T_lo)

                step = [0]

                def link(ins):
                    step[0] += 1
                    ins.then_inc(sem("gate_step"), 1)
                    dve.wait_ge(sem("gate_step"), step[0])

                tt, ts, red = nc.vector.tensor_tensor, nc.vector.tensor_scalar, nc.vector.tensor_reduce

                def over_e(c):
                    return c[:, :].unsqueeze(2).broadcast_to([P, TT, NE])

                dve.wait_ge(sem("bg_in"), 16)
                dve.wait_ge(sem("logits_made"), 1)
                link(tt(gate[:, :, :], bank(4)[:, 0:TT * NE].rearrange("p (t e) -> p t e", e=NE),
                        bgr[:, :].unsqueeze(1).broadcast_to([P, TT, NE]), ALU.add))
                link(red(col[:, :], gate[:, :, :], AX.X, ALU.max))
                tt(gate[:, :, :], gate[:, :, :], over_e(col), ALU.subtract).then_inc(sem("g_shifted"), 1)
                dve.wait_ge(sem("g_exp"), 1)
                link(red(col[:, :], gate[:, :, :], AX.X, ALU.add))
                link(nc.vector.reciprocal(col[:, :], col[:, :]))
                link(tt(gate[:, :, :], gate[:, :, :], over_e(col), ALU.mult))
                dve.wait_ge(sem("c_ready"), 5)
                link(nc.vector.tensor_copy(work[:, :, :], gate[:, :, :]))
                for hot in (hot1, hot2):
                    link(red(col[:, :], work[:, :, :], AX.X, ALU.max))
                    link(tt(key[:, :, :], work[:, :, :], over_e(col), ALU.is_equal))
                    link(tt(key[:, :, :], key[:, :, :], rev_e[:, :, :], ALU.mult))
                    link(red(col[:, :], key[:, :, :], AX.X, ALU.max))
                    link(tt(hot[:, :, :], key[:, :, :], over_e(col), ALU.is_equal))
                    if hot is hot1:
                        link(nc.vector.scalar_tensor_tensor(
                            out=work[:, :, :].rearrange("p t e -> p (t e)"),
                            in0=hot[:, :, :].rearrange("p t e -> p (t e)"), scalar=-2.0,
                            in1=work[:, :, :].rearrange("p t e -> p (t e)"), op0=ALU.mult, op1=ALU.add))
                link(tt(hot1[:, :, :], hot1[:, :, :], hot2[:, :, :], ALU.add))
                nc.vector.tensor_copy(chosen[:, :, :], hot1[:, :, :]).then_inc(sem("chosen_ready"), 1)
                link(tt(gate[:, :, :], gate[:, :, :], hot1[:, :, :], ALU.mult))
                link(red(col[:, :], gate[:, :, :], AX.X, ALU.add))
                link(ts(col[:, :], col[:, :], GATE_EPS, None, ALU.max))
                link(nc.vector.reciprocal(col[:, :], col[:, :]))
                tt(gate[:, :, :], gate[:, :, :], over_e(col), ALU.mult).then_inc(sem("gates_ready"), 1)
                dve.wait_ge(sem("gates_ready"), 1)

                dve.wait_ge(sem("ranks_made"), 1)
                link(ts(rank[:, :, :], bank(5)[:, 0:TT * NE].rearrange("p (t e) -> p t e", e=NE), FAR, None, ALU.add))
                link(tt(rank[:, :, :], rank[:, :, :], hot1[:, :, :], ALU.mult))
                link(ts(rank[:, :, :], rank[:, :, :], FAR, None, ALU.subtract))
                link(ts(cnt[:, :], bank(5)[:, TT * NE:(TT + 1) * NE], float(SLOTS), 1.0, ALU.is_gt, ALU.add))
                link(nc.vector.memset(start_at[:, 0:1], 0.0))
                for e in range(NE):
                    link(tt(start_at[:, e + 1:e + 2], start_at[:, e:e + 1], cnt[:, e:e + 1], ALU.add))
                link(nc.vector.tensor_copy(n_items[:, :], start_at[:, NE:NE + 1]))
                link(tt(in_e[:, :, :], iota_i[:, :, :],
                        start_at[:, 0:NE].unsqueeze(1).broadcast_to([P, ITEMS, NE]), ALU.is_ge))
                link(tt(tmp_i[:, :, :], iota_i[:, :, :],
                        start_at[:, 1:NE + 1].unsqueeze(1).broadcast_to([P, ITEMS, NE]), ALU.is_lt))
                link(tt(in_e[:, :, :], in_e[:, :, :], tmp_i[:, :, :], ALU.mult))
                link(tt(tmp_i[:, :, :], in_e[:, :, :], iota_e[:, :].unsqueeze(1).broadcast_to([P, ITEMS, NE]), ALU.mult))
                link(red(base[:, :], tmp_i[:, :, :], AX.X, ALU.add))
                link(nc.vector.tensor_copy(eid[:, :], base[:, :]))
                link(tt(tmp_i[:, :, :], iota_i[:, :, :],
                        start_at[:, 0:NE].unsqueeze(1).broadcast_to([P, ITEMS, NE]), ALU.subtract))
                link(tt(tmp_i[:, :, :], tmp_i[:, :, :], in_e[:, :, :], ALU.mult))
                link(red(base[:, :], tmp_i[:, :, :], AX.X, ALU.add))
                link(ts(base[:, :], base[:, :], float(SLOTS), None, ALU.mult))
                for t in range(TT):
                    for n, of in enumerate((rank, gate)):
                        link(tt(tmp_i[:, :, :], in_e[:, :, :], of[:, t, :].unsqueeze(1).broadcast_to([P, ITEMS, NE]),
                                ALU.mult))
                        link(red(table[:, :, n, t], tmp_i[:, :, :], AX.X, ALU.add))
                    link(tt(table[:, :, 0, t], table[:, :, 0, t], base[:, :], ALU.subtract))
                dve.wait_ge(sem("b1_turned"), 1)
                link(nc.vector.tensor_copy(b1T[:, :, :], bank(6)[:, 0:P].rearrange("p (e c) -> p e c", c=HC)))
                dve.wait_ge(sem("gT_turned"), 1)
                nc.vector.tensor_copy(gT[:, :], bank(7)[0:NE, :]).then_inc(sem("gT_ready"), 1)
                dve.wait_ge(sem("y_begun"), 1)
                dve.sem_inc(sem("wu_lo_done"), WLO_CREDIT)
                dve.sem_inc(sem("table_ready"), 1)

                items = items_of(dve)
                with dve.Fori(0, items) as i:
                    STEPS = 4
                    at = [0]

                    def link_item(ins):
                        at[0] += 1
                        ins.then_inc(sem("item_step"), 1)
                        dve.wait_ge(sem("item_step"), i * STEPS + at[0])

                    def unit_lo(v):
                        dve.wait_ge(sem("wu_hi_done"), i * UNITS + v + 1)
                        nc.vector.tensor_tensor(wu_lo[:, v % 4, :, :], wu_raw[:, v % 4, :, :],
                                                f32(wu_hi[:, v % 4, :, :]), ALU.subtract) \
                            .then_inc(sem("wu_lo_done"), 1)

                    e = dve.value_load(eid[0:1, bass.ds(i, 1)], min_val=0, max_val=NE - 1)
                    link_item(nc.vector.tensor_copy(cur[:, :, :], table[:, bass.ds(i, 1), :, :]
                                                    .rearrange("p a n t -> p (a n) t")))
                    nc.vector.tensor_copy(b1c[:, :], b1T[:, bass.ds(e, 1), :].rearrange("p a c -> p (a c)")) \
                        .then_inc(sem("b1_ready"), 1)
                    link_item(nc.vector.tensor_copy(gate2[:, :, 0], cur[:, 1, :]))
                    nc.vector.tensor_tensor(gate2[:, :, 1], cur[:, 1, :], f32(gate2[:, :, 0]), ALU.subtract)
                    for t in range(TT):
                        ins = nc.vector.tensor_scalar(sel[:, t, :], iota_s[:, :], cur[:, 0, t:t + 1], None,
                                                      ALU.is_equal)
                    ins.then_inc(sem("sel_ready"), 1)
                    unit_lo(0)
                    unit_lo(1)
                    for kk in range(2):
                        dve.wait_ge(sem("g_hi"), 2 * i + kk + 1)
                        nc.vector.tensor_tensor(gT_lo[:, 2 * kk:2 * kk + 2, :],
                                                psT[kk][:, :].rearrange("p (k s) -> p k s", s=SLOTS),
                                                f32(gT_hi[:, 2 * kk:2 * kk + 2, :]), ALU.subtract) \
                            .then_inc(sem("g_lo"), 1)
                    dve.wait_ge(sem("gs_made"), i + 1)
                    nc.vector.tensor_reduce(gs[:, :], psT[0][:, 0:2 * SLT].rearrange("p (s n) -> p s n", n=2),
                                            AX.X, ALU.add).then_inc(sem("gs_done"), 1)
                    unit_lo(2)
                    unit_lo(3)

                    def hidden(q):
                        for n in range(4 * q, 4 * q + 4):
                            dve.wait_ge(sem("h_made"), i * HC + n + 1)
                            if n == 4 * q and q >= 2:
                                dve.wait_ge(sem("l2_made"), L2_CREDIT + i * QT + q - 1)
                            nc.vector.tensor_copy(h_hi[:, q % 2, n % 4, :], hid[:, n % 2, :]) \
                                .then_inc(sem("h_hi_done"), 1)
                            dve.wait_ge(sem("h_hi_done"), i * HC + n + 1)
                            nc.vector.tensor_tensor(h_lo[:, q % 2, n % 4, :], hid[:, n % 2, :],
                                                    f32(h_hi[:, q % 2, n % 4, :]), ALU.subtract) \
                                .then_inc(sem("h_split"), 1)

                    hidden(0)
                    unit_lo(4)
                    hidden(1)
                    unit_lo(5)
                    hidden(2)
                    unit_lo(6)
                    hidden(3)
                    unit_lo(7)
                    for st in range(SLT):
                        dve.wait_ge(sem("eo_made"), i * SLT + st + 1)
                        link_item(nc.vector.tensor_copy(eo_hi[:, st, :], eo[:, st, :]))
                        nc.vector.tensor_tensor(eo_lo[:, st, :], eo[:, st, :], f32(eo_hi[:, st, :]), ALU.subtract) \
                            .then_inc(sem("eo_split"), 1)
                    assert at[0] == STEPS
                dve.wait_ge(sem("y_made"), 1)
                for t in range(TT):
                    nc.vector.tensor_tensor(x_sum[:, t, :], x_sum[:, t, :], bank(t), ALU.add).then_inc(sem("x_3"), 1)

            @block.tensor
            def _(pe):
                pe.sem_inc(sem("l1_made"), L1_CREDIT)
                pe.sem_inc(sem("l2_made"), L2_CREDIT)
                turn_tensor(pe, 3, xn3)
                pe.wait_ge(sem("turned3_lo"), KC)
                pe.wait_ge(sem("wg_lo"), 1)
                for t in range(TT):
                    cols = slice(t * P, (t + 1) * P)
                    ins = three(pe, bank(4)[:, t * NE:(t + 1) * NE],
                                [((x3T_hi[:, k, cols], x3T_lo[:, k, cols]), (Wg_hi[:, k, :], Wg_lo[:, k, :]))
                                 for k in range(KC)])
                ins.then_inc(sem("logits_made"), 1)
                pe.wait_ge(sem("b1_in"), 16)
                nc.tensor.matmul(bank(6)[:, 0:P], b1_raw[:, :], ident[:, :], is_transpose=True, start=True, stop=True) \
                    .then_inc(sem("b1_turned"), 1)
                pe.wait_ge(sem("chosen_ready"), 1)
                for t in range(TT):
                    for u in range(t + 1):
                        ins = nc.tensor.matmul(bank(5)[:, t * NE:(t + 1) * NE], (before if u == t else ones)[:, :],
                                               chosen[:, u, :], start=(u == 0), stop=(u == t))
                for u in range(TT):
                    ins = nc.tensor.matmul(bank(5)[:, TT * NE:(TT + 1) * NE], ones[:, :], chosen[:, u, :],
                                           start=(u == 0), stop=(u == TT - 1))
                ins.then_inc(sem("ranks_made"), 1)
                pe.wait_ge(sem("gates_ready"), 1)
                for t in range(TT):
                    ins = nc.tensor.matmul(bank(7)[0:NE, t * P:(t + 1) * P], gate[:, t, :], ident[:, :],
                                           is_transpose=True, start=True, stop=True)
                ins.then_inc(sem("gT_turned"), 1)
                pe.wait_ge(sem("gT_ready"), 1)
                pe.wait_ge(sem("b2_in"), 16)
                for t in range(TT):
                    ins = nc.tensor.matmul(bank(t), gT[:, t * P:(t + 1) * P], b2_sb[:, :], start=True, stop=False,
                                           skip_group_check=True)
                ins.then_inc(sem("y_begun"), 1)
                pe.wait_ge(sem("xg_lo"), 1)
                pe.wait_ge(sem("ident_r"), 1)
                pe.wait_ge(sem("table_ready"), 1)

                items = items_of(pe)
                with pe.Fori(0, items) as i:
                    pe.wait_ge(sem("sel_ready"), i + 1)
                    for k in range(KC):
                        dst = psT[k // 2][:, (k % 2) * SLOTS:(k % 2 + 1) * SLOTS]
                        for n, (t, part) in enumerate((t, part) for t in range(TT) for part in (xg_hi, xg_lo)):
                            ins = nc.tensor.matmul(dst, part[:, t, k * P:(k + 1) * P], sel[:, t, :],
                                                   start=(n == 0), stop=(n == 2 * TT - 1))
                        if k % 2:
                            ins.then_inc(sem("g_made"), 1)
                    for st in range(SLT):
                        slots = slice(st * P, (st + 1) * P)
                        for t in range(TT):
                            ins = nc.tensor.matmul(bank(6 + st)[:, t * P:(t + 1) * P].bitcast(FR), sel[:, t, slots],
                                                   ident_r[:, :], is_transpose=True, start=True, stop=True)
                        ins.then_inc(sem("selT_made"), 1)
                    pe.wait_ge(sem("g_lo"), 2 * i + 1)
                    for st in range(SLT):
                        slots = slice(st * P, (st + 1) * P)
                        for t in range(TT):
                            ins = nc.tensor.matmul(psT[0][:, 2 * st:2 * st + 2], sel[:, t, slots], gate2[:, t, :],
                                                   start=(t == 0), stop=(t == TT - 1))
                    ins.then_inc(sem("gs_made"), 1)
                    pe.wait_ge(sem("gs_done"), i + 1)
                    pe.wait_ge(sem("g_lo"), 2 * i + 2)

                    def layer1(q):
                        v = UNIT_OF[("1", q)]
                        pe.wait_ge(sem("wu_lo_done"), WLO_CREDIT + i * UNITS + v + 1)
                        for n in range(4 * q, 4 * q + 4):
                            if n >= 2:
                                pe.wait_ge(sem("h_made"), i * HC + n - 1)
                            cols = slice((n % 4) * P, (n % 4 + 1) * P)
                            three(pe, psT[n % 2][:, 0:SLOTS],
                                  [((wu_hi[:, v % 4, k, cols], wu_lo[:, v % 4, k, cols]),
                                    (gT_hi[:, k, :], gT_lo[:, k, :])) for k in range(KC)]) \
                                .then_inc(sem("l1_made"), 1)

                    def layer2(q):
                        v = UNIT_OF[("2", q)]
                        pe.wait_ge(sem("wu_lo_done"), WLO_CREDIT + i * UNITS + v + 1)
                        pe.wait_ge(sem("h_split"), i * HC + 4 * (q + 1))
                        if q == 0:
                            pe.wait_ge(sem("selT_done"), (i + 1) * SLT)
                        for st in range(SLT):
                            slots = slice(st * P, (st + 1) * P)
                            for c in range(4):
                                first, last = q == 0 and c == 0, q == QT - 1 and c == 3
                                hh, hl = h_hi[:, q % 2, c, slots], h_lo[:, q % 2, c, slots]
                                wh, wl = wu_hi[:, v % 4, c, :], wu_lo[:, v % 4, c, :]
                                nc.tensor.matmul(bank(6 + st), hh, wh, start=first, stop=False)
                                nc.tensor.matmul(bank(6 + st), hh, wl, start=False, stop=False)
                                ins = nc.tensor.matmul(bank(6 + st), hl, wh, start=False, stop=last)
                        ins.then_inc(sem("l2_made"), 1)

                    for which, q in UNIT_ORDER:
                        (layer1 if which == "1" else layer2)(q)
                    pe.wait_ge(sem("eo_split"), (i + 1) * SLT)
                    for t in range(TT):
                        for st in range(SLT):
                            for part in (eo_hi, eo_lo):
                                nc.tensor.matmul(bank(t), selT[:, st, t * P:(t + 1) * P], part[:, st, :],
                                                 start=False, stop=False, skip_group_check=True)
                pe.drain().then_inc(sem("y_made"), 1)


_INS = ['x', 'ctx_1024', 'L0_xattn_Wq', 'L0_xattn_bq', 'L0_xattn_Wkv', 'L0_xattn_bkv', 'L0_xattn_Wproj',
        'L0_xattn_bproj', 'L0_attn_WQ', 'L0_attn_WK', 'L0_attn_WV_down', 'L0_attn_WV_up', 'L0_ffn_Wg', 'L0_ffn_bg',
        'L0_ffn_W1', 'L0_ffn_b1', 'L0_ffn_W2', 'L0_ffn_b2']
_OUTS = [((8, 64, 512), 'float32')]


def kernel(**inputs):
    import numpy as _np
    import concourse.bacc as _bacc
    from concourse import mybir as _mybir
    from concourse.bass_utils import run_bass_kernel_spmd as _run

    nc = _bacc.Bacc("TRN2", target_bir_lowering=False, num_devices=1)
    arrays, args = {}, []
    for name in _INS:
        a = _np.ascontiguousarray(inputs[name])
        arrays[f"in_{name}_dram"] = a
        args.append(nc.dram_tensor(f"in_{name}_dram", a.shape, _mybir.dt.from_np(a.dtype), kind="ExternalInput").ap())
    for i, (shape, dtype) in enumerate(_OUTS):
        dt = _mybir.dt.from_np(_np.dtype(dtype))
        args.append(nc.dram_tensor(f"out_{i}_dram", shape, dt, kind="ExternalOutput").ap())
    perceiver_kernel(nc, *args)
    r = _run(nc, [arrays], core_ids=[0])
    got = tuple(r.results[0][f"out_{i}_dram"] for i in range(len(_OUTS)))
    return got[0]
```

```python
from contextlib import ExitStack

import concourse.bass as bass
from concourse import mybir
from concourse.alu_op_type import AluOpType as ALU

ACT = mybir.ActivationFunctionType
F32 = mybir.dt.float32
FR = mybir.dt.float32r
BF16 = mybir.dt.bfloat16
I32 = mybir.dt.int32
AX = mybir.AxisListType



def f32(ap):
    return ap.bitcast(F32)


def perceiver_kernel(nc, x_in, ctx_in, Wq, bq, Wkv, bkv, Wproj, bproj,
                     WQ, WK, WVd, WVu, Wg, bg, W1, b1, W2, b2, out):
    B, S, D = x_in.shape
    CK = ctx_in.shape[1]
    P = 128
    T = B * S
    TT = T // P
    KC = D // P
    NH = 16
    HD = D // NH
    NP = NH // 2
    QK_SCALE = HD ** -0.5
    NT = -(-CK // P)
    TAIL = CK - (NT - 1) * P
    KEYS = CK + CK % 2
    GROUPS = [(2 * g, 2) for g in range(NT // 2)]
    GROUPS[-1] = (GROUPS[-1][0], NT - GROUPS[-1][0])
    NG = len(GROUPS)
    GMAX = KEYS - GROUPS[-1][0] * P
    assert NG % 2 == 0 and T == 512 and D == 512 and GMAX <= 512
    S0 = 2 * ((4 * 512 - KEYS) // 4)
    S_PARTS = [(max(0, 512 * c - S0), min(KEYS, 512 * (c + 1) - S0)) for c in range(4)]
    assert min(b - a for a, b in S_PARTS) >= 256
    S_HALVES = [(0, S_PARTS[1][1]), (S_PARTS[2][0], CK)]
    KV_USES = NG * KC + NT
    PT_GROUPS = NT // 4
    assert NT == 4 * PT_GROUPS + 1 and PT_GROUPS == 3
    EPS = 1e-5

    x_rows = x_in.rearrange("b s d -> (b s) d").rearrange("(t p) d -> p t d", p=P)
    out_rows = out.rearrange("b s d -> (b s) d").rearrange("(t p) d -> p t d", p=P)

    q_dram = [nc.dram_tensor(f"qd_{part}", [D, T], F32, kind="Internal").ap() for part in ("hi", "lo")]
    r_dram = nc.dram_tensor("inverse_sums", [2, NP, T], F32, kind="Internal").ap()
    o_dram = nc.dram_tensor("o_heads", [NP, P, T], F32, kind="Internal").ap()

    with ExitStack() as whole:
        sems = {}

        def sem(name):
            if name not in sems:
                sems[name] = whole.enter_context(nc.semaphore(name))
            return sems[name]

        def sb(scope, name, shape, dt=F32):
            return scope.enter_context(nc.sbuf_tensor(name, shape, dt))

        def ps(name, shape):
            return whole.enter_context(nc.psum_tensor(name, shape, F32))

        psS = ps("ps_scores", [P, 4, 512])
        psS_row = psS[:, :, :].rearrange("p a c -> p (a c)")
        psT = [ps(f"ps_turn{i}", [P, 512]) for i in range(3)]
        psO = ps("ps_out", [P, 512])

        def bank(i):
            return psS[:, i, :] if i < 4 else (psT + [psO])[i - 4][:, :]

        ident = sb(whole, "ident", [P, P])
        ident_r = sb(whole, "ident_r", [P, P], FR)

        def norm_vector(dve, n, x, xn, tmp):
            done = sem("ln_step")
            at = [7 * (n - 1)]

            def link(ins):
                at[0] += 1
                ins.then_inc(done, 1)
                dve.wait_ge(done, at[0])
            stats, mv, ve, root, rs = tmp
            for t in range(TT):
                ins = nc.vector.bn_stats(stats[:, t, :], x[:, t, :])
            link(ins)
            for t in range(TT):
                ins = nc.vector.bn_aggr(mv[:, t, :], stats[:, t, :])
            link(ins)
            nc.vector.tensor_scalar(ve[:, :], mv[:, :, 1], EPS, None, ALU.add).then_inc(sem("ln_var"), 1)
            dve.wait_ge(sem("ln_root"), n)
            link(nc.vector.reciprocal(root[:, :], root[:, :]))
            link(nc.vector.tensor_tensor(rs[:, :], root[:, :], root[:, :], ALU.mult))
            link(nc.vector.tensor_tensor(rs[:, :], rs[:, :], ve[:, :], ALU.mult))
            link(nc.vector.tensor_scalar(rs[:, :], rs[:, :], -0.5, 1.5, ALU.mult, ALU.add))
            link(nc.vector.tensor_tensor(rs[:, :], rs[:, :], root[:, :], ALU.mult))
            for t in range(TT):
                ins = nc.vector.tensor_scalar(xn[:, t, :], x[:, t, :], mv[:, t, 0:1], rs[:, t:t + 1],
                                              ALU.subtract, ALU.mult)
            ins.then_inc(sem("ln_done"), 1)
            assert at[0] == 7 * n

        def norm_scalar(act, n, tmp):
            act.wait_ge(sem("ln_var"), n)
            nc.scalar.activation(tmp[3][:, :], tmp[2][:, :], ACT.Sqrt).then_inc(sem("ln_root"), 1)

        def turn_tensor(pe, n, xn):
            pe.wait_ge(sem("ln_done"), n)
            for k in range(KC):
                for t in range(TT):
                    ins = nc.tensor.matmul(bank(k)[:, t * P:(t + 1) * P], xn[:, t, k * P:(k + 1) * P],
                                           ident[:, :], is_transpose=True, start=True, stop=True)
                ins.then_inc(sem("x_turned"), 1)

        def turn_scalar(act, n, hi):
            for k in range(KC):
                act.wait_ge(sem("x_turned"), KC * (n - 1) + k + 1)
                nc.scalar.copy(hi[:, k, :], bank(k)).then_inc(sem("x_turned_hi"), 1)

        def turn_vector(dve, n, hi, lo):
            for k in range(KC):
                dve.wait_ge(sem("x_turned_hi"), KC * (n - 1) + k + 1)
                nc.vector.tensor_tensor(lo[:, k, :], bank(k), f32(hi[:, k, :]), ALU.subtract) \
                    .then_inc(sem("x_turned_lo"), 1)

        def three(pe, out_ap, pairs):
            last = None
            for i, ((sh, sl), (mh, ml)) in enumerate(pairs):
                nc.tensor.matmul(out_ap, sh, mh, start=(i == 0), stop=False)
                nc.tensor.matmul(out_ap, sh, ml, start=False, stop=False)
                last = nc.tensor.matmul(out_ap, sl, mh, start=False, stop=(i == len(pairs) - 1))
            return last

        scope = ExitStack()
        Wkv_hi = sb(scope, "Wkv_hi", [P, KC, 2 * D], FR)
        Wkv_lo = sb(scope, "Wkv_lo", [P, KC, 2 * D], FR)
        bkc = sb(scope, "bkc", [64, NP])
        raw = sb(scope, "raw", [P, 5, D])
        cT_hi = sb(scope, "cT_hi", [P, KC, 2 * P + GMAX], FR)
        cT_lo = sb(scope, "cT_lo", [P, KC, 2 * P + GMAX], FR)
        Qs_hi = sb(scope, "Qs_hi", [P, NP, P], FR)
        Qs_lo = sb(scope, "Qs_lo", [P, NP, P], FR)
        Pr = sb(scope, "Pr", [P, 3, CK])
        PT = sb(scope, "PT", [P, NT, 2, P], FR)
        U = sb(scope, "U", [P, NP, P])
        negmax = sb(scope, "negmax", [P, NP])
        halfmax = sb(scope, "halfmax", [P, NP, 2])
        half_sum = sb(scope, "half_sum", [P, NP, 2])
        total = sb(scope, "total", [P, NP, B])
        rinvT = sb(scope, "rinvT", [B * NP, P])
        prep = ExitStack()
        x_tok = sb(prep, "x_tok", [P, TT, D])
        xn = sb(prep, "xn", [P, TT, D])
        xT_hi = sb(prep, "xT_hi", [P, KC, T], FR)
        xT_lo = sb(prep, "xT_lo", [P, KC, T], FR)
        Wq_raw = sb(prep, "Wq_raw", [P, KC, D])
        Wq_hi = sb(prep, "Wq_hi", [P, KC, D], FR)
        Wq_lo = sb(prep, "Wq_lo", [P, KC, D], FR)
        bqc = sb(prep, "bqc", [P, KC])
        Wkv_raw = sb(prep, "Wkv_raw", [P, KC, 2 * D])
        q_sb = sb(prep, "q_sb", [P, KC, T])
        q_hi = sb(prep, "q_hi", [P, KC, T], FR)
        q_lo = sb(prep, "q_lo", [P, KC, T], FR)
        lnt1 = (sb(prep, "st1", [P, TT, 6]), sb(prep, "mv1", [P, TT, 2]), sb(prep, "ve1", [P, TT]),
                sb(prep, "rt1", [P, TT]), sb(prep, "rs1", [P, TT]))
        prep.close()
        Ks = sb(scope, "Ks", [P, NP, KEYS], FR)
        Vs = sb(scope, "Vs", [P, NT, NP, P], FR)
        scope.close()

        def uses_through(g):
            return sum(KC + n for _, n in GROUPS[:g + 1])

        def tile_rows(c):
            return TAIL if c == NT - 1 else P

        def group_cols(g):
            return (KEYS if g == NG - 1 else (GROUPS[g][0] + GROUPS[g][1]) * P) - GROUPS[g][0] * P

        with nc.Block() as block:

            def load_group(sp, b, g):
                c0, n = GROUPS[g]
                full = n if g < NG - 1 else n - 1
                src = ctx_in[bass.ds(b, 1), :, :].rearrange("a k d -> (a k) d")
                sp.dma_start(raw[:, 2 * (g % 2):2 * (g % 2) + full, :],
                             src[c0 * P:(c0 + full) * P, :].rearrange("(t p) d -> p t d", p=P)) \
                    .then_inc(sem(f"raw_in{g % 2}"), 16)
                if g == NG - 1:
                    sp.dma_start(raw[0:TAIL, 2 * (g % 2) + full, :], src[(c0 + full) * P:CK, :]) \
                        .then_inc(sem(f"raw_in{g % 2}"), 16)

            RAW_PER_BATCH = [16 * (NG // 2), 16 * (NG // 2 + 1)]

            def load_queries(sp, b):
                for part, dst in enumerate((Qs_hi, Qs_lo)):
                    src = q_dram[part].rearrange("(j h r) t -> h r j t", h=2, r=HD)
                    for h in range(2):
                        for twice in range(2):
                            r0 = 64 * twice + HD * h
                            sp.dma_start(f32(dst[r0:r0 + HD, :, S * h:S * (h + 1)]),
                                         src[h][:, :, bass.ds(b * S, S)]).then_inc(sem("q_in"), 16)

            def store_outputs(sp, b):
                for twice in range(2):
                    for h in range(2):
                        r0 = 64 * twice + HD * h
                        sp.dma_start(o_dram[:, r0:r0 + HD, bass.ds(b * S, S)].rearrange("j r t -> r j t"),
                                     U[r0:r0 + HD, :, S * h:S * (h + 1)]).then_inc(sem("u_free"), 16)

            @block.sync
            def _(sp):
                sp.dma_start(x_tok[:, :, :], x_rows).then_inc(sem("x_in"), 16)
                sp.dma_start(Wq_raw[:, :, :], Wq.rearrange("(k p) n -> p k n", p=P)).then_inc(sem("wq_in"), 16)
                sp.dma_start(bqc[:, :], bq.rearrange("(m p) -> p m", p=P), allow_slow_non_contiguous=True).then_inc(sem("bq_in"), 16)
                sp.dma_start(bkc[:, :], bkv[0:D].rearrange("(j r) -> r j", r=64), allow_slow_non_contiguous=True).then_inc(sem("bk_in"), 16)
                sp.dma_start(Wkv_raw[:, :, :], Wkv.rearrange("(k p) n -> p k n", p=P)).then_inc(sem("wkv_in"), 16)
                load_group(sp, 0, 0)
                load_group(sp, 0, 1)
                sp.wait_ge(sem("q_split"), 4)
                sp.dma_start(q_dram[0].rearrange("(m p) t -> p m t", p=P), f32(q_hi[:, :, :])).then_inc(sem("q_out"), 16)
                sp.dma_start(q_dram[1].rearrange("(m p) t -> p m t", p=P), f32(q_lo[:, :, :])).then_inc(sem("q_out"), 16)
                sp.wait_ge(sem("q_out"), 32)
                sp.wait_ge(sem("q_zeroed"), 2)
                load_queries(sp, 0)
                sp.sem_inc(sem("u_free"), 1)

                def loads_of_batch(b, last):
                    for g in range(NG):
                        if last and g + 2 >= NG:
                            break
                        sp.wait_ge(sem("c_turned"), b * (NG * KC) + KC * (g + 1))
                        load_group(sp, b + (g + 2) // NG, (g + 2) % NG)
                    if not last:
                        sp.wait_ge(sem("s_made"), (b + 1) * 2 * NP)
                        load_queries(sp, b + 1)
                    sp.wait_ge(sem("o_summed"), (b + 1) * NP)
                    store_outputs(sp, b)

                with sp.Fori(0, B - 1) as b:
                    loads_of_batch(b, False)
                loads_of_batch(B - 1, True)
                sp.wait_ge(sem("r_turned"), 1)
                sp.dma_start(r_dram.rearrange("h j (b t) -> (j b) h t", t=S), rinvT[:, :].rearrange("p (h t) -> p h t", h=2)) \
                    .then_inc(sem("r_out"), 16)
                sp.wait_ge(sem("r_out"), 16)
                sp.wait_ge(sem("u_free"), 64 * B + 1)

            @block.gpsimd
            def _(pool):
                nc.gpsimd.memset(ident[:, :], 0.0).then_inc(sem("ident0"), 1)
                pool.wait_ge(sem("ident0"), 1)
                nc.gpsimd.affine_select(out=ident[:, :], in_=ident[:, :], compare_op=ALU.not_equal, fill=1.0,
                                        base=0, pattern=[[-1, P]], channel_multiplier=1) \
                    .then_inc(sem("ident_ready"), 1)
                nc.gpsimd.memset(f32(Qs_hi[:, :, :]), 0.0).then_inc(sem("q_zeroed"), 1)
                nc.gpsimd.memset(f32(Qs_lo[:, :, :]), 0.0).then_inc(sem("q_zeroed"), 1)
                nc.gpsimd.memset(f32(cT_hi[:, :, 2 * P + GMAX - 1:2 * P + GMAX]), 0.0).then_inc(sem("pad_zeroed"), 1)
                nc.gpsimd.memset(f32(cT_lo[:, :, 2 * P + GMAX - 1:2 * P + GMAX]), 0.0).then_inc(sem("pad_zeroed"), 1)

            @block.scalar
            def _(act):
                norm_scalar(act, 1, lnt1)
                act.wait_ge(sem("wq_in"), 16)
                nc.scalar.copy(Wq_hi[:, :, :], Wq_raw[:, :, :]).then_inc(sem("wq_hi"), 1)
                turn_scalar(act, 1, xT_hi)
                act.wait_ge(sem("wkv_in"), 16)
                nc.scalar.copy(Wkv_hi[:, :, :], Wkv_raw[:, :, :]).then_inc(sem("wkv_hi"), 1)
                for m in range(KC):
                    act.wait_ge(sem("q_scaled"), m + 1)
                    nc.scalar.copy(q_hi[:, m, :], q_sb[:, m, :]).then_inc(sem("q_hi"), 1)
                act.wait_ge(sem("bk_in"), 16)

                with act.Fori(0, B) as b:
                    def turn_hi(g):
                        c0, n = GROUPS[g]
                        cols = CK - c0 * P if g == NG - 1 else n * P
                        at = 2 * P * (g % 2)
                        if g >= 2:
                            act.wait_ge(sem("kv_made"), b * KV_USES + uses_through(g - 2))
                        for k in range(KC):
                            act.wait_ge(sem("c_turned"), b * (NG * KC) + g * KC + k + 1)
                            nc.scalar.copy(cT_hi[:, k, at:at + cols], psT[(g * KC + k) % 3][:, 0:cols]) \
                                .then_inc(sem("c_hi"), 1)

                    use = 0
                    turn_hi(0)
                    for g in range(NG):
                        if g + 1 < NG:
                            turn_hi(g + 1)
                        c0, n = GROUPS[g]
                        gc = group_cols(g)
                        for m in range(KC):
                            act.wait_ge(sem("kv_made"), b * KV_USES + use + 1)
                            for h in range(2):
                                j = 2 * m + h
                                ins = nc.scalar.activation(Ks[0:64, j, c0 * P:c0 * P + gc],
                                                           psS[64 * h:64 * h + 64, use % 4, 0:gc], ACT.Identity,
                                                           bias=bkc[:, j:j + 1])
                            ins.then_inc(sem("kv_hi"), 1)
                            use += 1
                        for c in range(c0, c0 + n):
                            act.wait_ge(sem("kv_made"), b * KV_USES + use + 1)
                            M = tile_rows(c)
                            nc.scalar.copy(Vs[0:M, c, :, 0:64],
                                           psS[0:M, use % 4, :].rearrange("p (j r) -> p j r", r=64)) \
                                .then_inc(sem("kv_hi"), 1)
                            use += 1

                    def exps(j):
                        act.wait_ge(sem("s_max"), b * NP + j + 1)
                        if j >= 3:
                            act.wait_ge(sem("tail_turned"), b * NP + j - 2)
                        for half, (k0, k1) in enumerate(S_HALVES):
                            nc.scalar.activation(Pr[:, j % 3, k0:k1], psS_row[:, S0 + k0:S0 + k1], ACT.Exp,
                                                 bias=negmax[:, j:j + 1], accum_out=half_sum[:, j, half:half + 1]) \
                                .then_inc(sem("p_exp"), 1)

                    def turned_hi(j, q):
                        if j >= 1:
                            act.wait_ge(sem("o_part"), b * (NP * PT_GROUPS) + (j - 1) * PT_GROUPS + q + 1)
                        act.wait_ge(sem(f"p_turned{q}"), b * NP + j + 1)
                        nc.scalar.copy(PT[:, 4 * q:4 * q + 4, 0, :],
                                       psT[q][:, :].rearrange("p (c r) -> p c r", r=P)).then_inc(sem(f"pt_hi{q}"), 1)

                    def tail_hi(j):
                        if j >= 1:
                            act.wait_ge(sem("o_made"), b * NP + j)
                        act.wait_ge(sem("tail_turned"), b * NP + j + 1)
                        nc.scalar.copy(PT[0:TAIL, NT - 1, 0, :], psO[0:TAIL, 2 * P:3 * P]).then_inc(sem("tail_hi"), 1)

                    for j in range(NP + 2):
                        if j < NP:
                            exps(j)
                        if j >= 2:
                            tail_hi(j - 2)
                            turned_hi(j - 2, 2)
                        if 1 <= j <= NP:
                            turned_hi(j - 1, 0)
                            turned_hi(j - 1, 1)
                act.wait_ge(sem("r_made"), 1)
                nc.scalar.copy(rinvT[:, :], bank(4)[0:B * NP, 0:P]).then_inc(sem("r_turned"), 1)

            @block.vector
            def _(dve):
                dve.wait_ge(sem("x_in"), 16)
                norm_vector(dve, 1, x_tok, xn, lnt1)
                dve.wait_ge(sem("wq_hi"), 1)
                nc.vector.tensor_tensor(Wq_lo[:, :, :], Wq_raw[:, :, :], f32(Wq_hi[:, :, :]), ALU.subtract) \
                    .then_inc(sem("wq_lo"), 1)
                turn_vector(dve, 1, xT_hi, xT_lo)
                dve.wait_ge(sem("bq_in"), 16)
                for m in range(KC):
                    dve.wait_ge(sem("q_made"), m + 1)
                    nc.vector.tensor_scalar(q_sb[:, m, :], bank(4 + m), bqc[:, m:m + 1], QK_SCALE,
                                            ALU.add, ALU.mult).then_inc(sem("q_scaled"), 1)
                for m in range(KC):
                    dve.wait_ge(sem("q_hi"), m + 1)
                    nc.vector.tensor_tensor(q_lo[:, m, :], q_sb[:, m, :], f32(q_hi[:, m, :]), ALU.subtract) \
                        .then_inc(sem("q_split"), 1)
                dve.wait_ge(sem("wkv_hi"), 1)
                nc.vector.tensor_tensor(Wkv_lo[:, :, :], Wkv_raw[:, :, :], f32(Wkv_hi[:, :, :]), ALU.subtract) \
                    .then_inc(sem("wkv_lo"), 1)
                dve.wait_ge(sem("q_out"), 32)
                dve.wait_ge(sem("bk_in"), 16)

                with dve.Fori(0, B) as b:
                    def turn_lo(g):
                        c0, n = GROUPS[g]
                        cols = CK - c0 * P if g == NG - 1 else n * P
                        at = 2 * P * (g % 2)
                        for k in range(KC):
                            dve.wait_ge(sem("c_hi"), b * (NG * KC) + g * KC + k + 1)
                            nc.vector.tensor_tensor(cT_lo[:, k, at:at + cols], psT[(g * KC + k) % 3][:, 0:cols],
                                                    f32(cT_hi[:, k, at:at + cols]), ALU.subtract) \
                                .then_inc(sem("c_lo"), 1)

                    use = 0
                    turn_lo(0)
                    for g in range(NG):
                        if g + 1 < NG:
                            turn_lo(g + 1)
                        c0, n = GROUPS[g]
                        gc = group_cols(g)
                        for m in range(KC):
                            dve.wait_ge(sem("kv_hi"), b * KV_USES + use + 1)
                            for h in range(2):
                                j = 2 * m + h
                                cols = slice(c0 * P, c0 * P + gc)
                                ins = nc.vector.scalar_tensor_tensor(
                                    out=Ks[64:128, j, cols], in0=psS[64 * h:64 * h + 64, use % 4, 0:gc],
                                    scalar=bkc[:, j:j + 1], in1=f32(Ks[0:64, j, cols]),
                                    op0=ALU.add, op1=ALU.subtract)
                            ins.then_inc(sem("kv_lo"), 1)
                            use += 1
                        for c in range(c0, c0 + n):
                            dve.wait_ge(sem("kv_hi"), b * KV_USES + use + 1)
                            M = tile_rows(c)
                            nc.vector.tensor_tensor(Vs[0:M, c, :, 64:128],
                                                    psS[0:M, use % 4, :].rearrange("p (j r) -> p j r", r=64),
                                                    f32(Vs[0:M, c, :, 0:64]), ALU.subtract) \
                                .then_inc(sem("kv_lo"), 1)
                            use += 1

                    def half_max(j, half):
                        k0, k1 = S_HALVES[half]
                        dve.wait_ge(sem("s_made"), (b * NP + j) * 2 + half + 1)
                        nc.vector.tensor_reduce(halfmax[:, j, half:half + 1], psS_row[:, S0 + k0:S0 + k1],
                                                AX.X, ALU.max, negate=True).then_inc(sem("half_max"), 1)

                    def row_max(j):
                        dve.wait_ge(sem("half_max"), (b * NP + j) * 2 + 2)
                        nc.vector.tensor_reduce(negmax[:, j:j + 1], halfmax[:, j, :], AX.X, ALU.min) \
                            .then_inc(sem("s_max"), 1)

                    def turned_lo(j, q):
                        dve.wait_ge(sem(f"pt_hi{q}"), b * NP + j + 1)
                        nc.vector.tensor_tensor(PT[:, 4 * q:4 * q + 4, 1, :],
                                                psT[q][:, :].rearrange("p (c r) -> p c r", r=P),
                                                f32(PT[:, 4 * q:4 * q + 4, 0, :]), ALU.subtract) \
                            .then_inc(sem(f"pt_lo{q}"), 1)

                    def tail_lo(j):
                        dve.wait_ge(sem("tail_hi"), b * NP + j + 1)
                        nc.vector.tensor_tensor(PT[0:TAIL, NT - 1, 1, :], psO[0:TAIL, 2 * P:3 * P],
                                                f32(PT[0:TAIL, NT - 1, 0, :]), ALU.subtract) \
                            .then_inc(sem("tail_lo"), 1)

                    def out_sum(j):
                        dve.wait_ge(sem("o_made"), b * NP + j + 1)
                        if j == 0:
                            dve.wait_ge(sem("u_free"), b * 64 + 1)
                        nc.vector.tensor_reduce(U[:, j, :], psO[:, 0:2 * P].rearrange("p (a r) -> p r a", a=2),
                                                AX.X, ALU.add).then_inc(sem("o_summed"), 1)

                    half_max(0, 0)
                    half_max(0, 1)
                    row_max(0)
                    for j in range(NP + 2):
                        if j >= 2:
                            turned_lo(j - 2, 0)
                            turned_lo(j - 2, 1)
                        if j >= 3:
                            out_sum(j - 3)
                        if j + 1 < NP:
                            half_max(j + 1, 0)
                        if j >= 2:
                            tail_lo(j - 2)
                            turned_lo(j - 2, 2)
                        if j + 1 < NP:
                            half_max(j + 1, 1)
                            row_max(j + 1)
                    dve.wait_ge(sem("p_exp"), (b + 1) * 2 * NP)
                    nc.vector.tensor_tensor(total[:, :, bass.ds(b, 1)].rearrange("p j a -> p (j a)"),
                                            half_sum[:, :, 0], half_sum[:, :, 1], ALU.add).then_inc(sem("totals"), 1)
                    out_sum(NP - 1)
                dve.wait_ge(sem("totals"), B)
                nc.vector.reciprocal(total[:, :, :], total[:, :, :]).then_inc(sem("r_inverse"), 1)

            @block.tensor
            def _(pe):
                pe.wait_ge(sem("ident_ready"), 1)
                turn_tensor(pe, 1, xn)
                pe.wait_ge(sem("wq_lo"), 1)
                pe.wait_ge(sem("x_turned_lo"), 1 * KC)
                for m in range(KC):
                    cols = slice(m * P, (m + 1) * P)
                    three(pe, bank(4 + m), [((Wq_hi[:, k, cols], Wq_lo[:, k, cols]), (xT_hi[:, k, :], xT_lo[:, k, :]))
                                            for k in range(KC)]).then_inc(sem("q_made"), 1)
                pe.wait_ge(sem("q_scaled"), KC)
                pe.wait_ge(sem("wkv_lo"), 1)
                pe.wait_ge(sem("pad_zeroed"), 2)

                with pe.Fori(0, B) as b:
                    def turn(g):
                        c0, n = GROUPS[g]
                        pe.wait_ge(sem(f"raw_in{g % 2}"),
                                   b * RAW_PER_BATCH[g % 2] + (16 * (g // 2 + 1) if g < NG - 1 else RAW_PER_BATCH[1]))
                        for k in range(KC):
                            if g * KC + k >= 3:
                                pe.wait_ge(sem("c_lo"), b * (NG * KC) + g * KC + k - 2)
                            for i in range(n):
                                M = tile_rows(c0 + i)
                                ins = nc.tensor.matmul(psT[(g * KC + k) % 3][:, i * P:i * P + M],
                                                       raw[0:M, 2 * (g % 2) + i, k * P:(k + 1) * P], ident[0:M, 0:M],
                                                       is_transpose=True, start=True, stop=True)
                            ins.then_inc(sem("c_turned"), 1)

                    use = 0
                    turn(0)
                    for g in range(NG):
                        if g + 1 < NG:
                            turn(g + 1)
                        c0, n = GROUPS[g]
                        gc = group_cols(g)
                        at = 2 * P * (g % 2)
                        pe.wait_ge(sem("c_lo"), b * (NG * KC) + KC * (g + 1))
                        for m in range(KC):
                            if use >= 4:
                                pe.wait_ge(sem("kv_lo"), b * KV_USES + use - 3)
                            cols = slice(m * P, (m + 1) * P)
                            three(pe, psS[:, use % 4, 0:gc],
                                  [((Wkv_hi[:, k, cols], Wkv_lo[:, k, cols]),
                                    (cT_hi[:, k, at:at + gc], cT_lo[:, k, at:at + gc])) for k in range(KC)]) \
                                .then_inc(sem("kv_made"), 1)
                            use += 1
                        for c in range(c0, c0 + n):
                            pe.wait_ge(sem("kv_lo"), b * KV_USES + use - 3)
                            M = tile_rows(c)
                            rows = slice(at + (c - c0) * P, at + (c - c0) * P + M)
                            ins = three(pe, psS[0:M, use % 4, :],
                                        [((cT_hi[:, k, rows], cT_lo[:, k, rows]),
                                          (Wkv_hi[:, k, D:2 * D], Wkv_lo[:, k, D:2 * D])) for k in range(KC)])
                            ins.then_inc(sem("kv_made"), 1)
                            use += 1

                    def scores(j, half):
                        if j >= 1:
                            pe.wait_ge(sem("p_exp"), (b * NP + j - 1) * 2 + half + 1)
                        for part, Q in enumerate((Qs_hi, Qs_lo)):
                            for k0, k1 in S_PARTS[2 * half:2 * half + 2]:
                                ins = nc.tensor.matmul(psS_row[:, S0 + k0:S0 + k1], Q[:, j, :], Ks[:, j, k0:k1],
                                                       start=(part == 0), stop=(part == 1))
                        ins.then_inc(sem("s_made"), 1)

                    def turn_probs(j, q):
                        pe.wait_ge(sem("p_exp"), (b * NP + j + 1) * 2)
                        if j >= 1:
                            pe.wait_ge(sem(f"pt_lo{q}"), b * NP + j)
                        for i in range(4):
                            c = 4 * q + i
                            ins = nc.tensor.matmul(psT[q][:, i * P:(i + 1) * P], Pr[:, j % 3, c * P:(c + 1) * P],
                                                   ident[:, :], is_transpose=True, start=True, stop=True)
                        ins.then_inc(sem(f"p_turned{q}"), 1)

                    def turn_tail(j):
                        if j >= 1:
                            pe.wait_ge(sem("o_summed"), b * NP + j)
                        nc.tensor.matmul(psO[0:TAIL, 2 * P:3 * P], Pr[:, j % 3, CK - TAIL:CK], ident[:, :],
                                         is_transpose=True, start=True, stop=True).then_inc(sem("tail_turned"), 1)

                    def outputs(j):
                        pe.wait_ge(sem("tail_lo"), b * NP + j + 1)
                        for c in range(NT):
                            if c % 4 == 0 and c < NT - 1:
                                pe.wait_ge(sem(f"pt_lo{c // 4}"), b * NP + j + 1)
                            M = tile_rows(c)
                            ins = nc.tensor.matmul(psO[:, 0:2 * P], Vs[0:M, c, j, :],
                                                   PT[0:M, c, :, :].rearrange("p a r -> p (a r)"),
                                                   start=(c == 0), stop=(c == NT - 1))
                            if c % 4 == 3:
                                ins.then_inc(sem("o_part"), 1)
                        ins.then_inc(sem("o_made"), 1)

                    pe.wait_ge(sem("kv_lo"), (b + 1) * KV_USES)
                    pe.wait_ge(sem("q_in"), (b + 1) * 128)
                    scores(0, 0)
                    scores(0, 1)
                    for j in range(NP + 2):
                        if 1 <= j <= NP:
                            turn_probs(j - 1, 0)
                        if j + 1 < NP:
                            scores(j + 1, 0)
                        if j >= 2:
                            turn_tail(j - 2)
                        if 1 <= j <= NP:
                            turn_probs(j - 1, 1)
                        if j + 1 < NP:
                            scores(j + 1, 1)
                        if j >= 2:
                            outputs(j - 2)
                        if 1 <= j <= NP:
                            turn_probs(j - 1, 2)
                pe.wait_ge(sem("r_inverse"), 1)
                nc.tensor.matmul(bank(4)[0:B * NP, 0:P], total[:, :, :].rearrange("p j b -> p (j b)"), ident[:, :],
                                 is_transpose=True, start=True, stop=True).then_inc(sem("r_made"), 1)

        SH, SD = WQ.shape[0], WQ.shape[2]
        HH = SH // 2
        HP = HH // 2
        FMIN = -3.4028234663852886e38
        SG = HH * TT

        late = whole.enter_context(ExitStack())
        x_sum = sb(late, "x_sum", [P, TT, D])
        scope = ExitStack()
        xn2 = sb(scope, "xn2", [P, TT, D])
        x2T_hi = sb(scope, "x2T_hi", [P, KC, T], FR)
        x2T_lo = sb(scope, "x2T_lo", [P, KC, T], FR)
        lnt2 = (sb(scope, "st2", [P, TT, 6]), sb(scope, "mv2", [P, TT, 2]), sb(scope, "ve2", [P, TT]),
                sb(scope, "rt2", [P, TT]), sb(scope, "rs2", [P, TT]))
        triu = sb(scope, "triu", [P, 2, SD])
        diag = sb(scope, "diag", [P, SD])
        proj = ExitStack()
        oT = sb(proj, "oT", [P, NP, T])
        oR = sb(proj, "oR", [P, NP, T])
        oT_hi = sb(proj, "oT_hi", [P, NP, T], FR)
        oT_lo = sb(proj, "oT_lo", [P, NP, T], FR)
        Wp_raw = sb(proj, "Wp_raw", [P, NP, D])
        Wp_hi = sb(proj, "Wp_hi", [P, NP, D], FR)
        Wp_lo = sb(proj, "Wp_lo", [P, NP, D], FR)
        bvc = sb(proj, "bvc", [P, NP])
        bpr = sb(proj, "bpr", [P, D])
        proj.close()
        W2_raw = sb(scope, "sW_raw", [P, 2, KC, HH * SD])
        W2_hi = sb(scope, "sW_hi", [P, 2, KC, HH * SD], FR)
        W2_lo = sb(scope, "sW_lo", [P, 2, KC, HH * SD], FR)
        QT_hi = sb(scope, "QT_hi", [P, HP, T], FR)
        QT_lo = sb(scope, "QT_lo", [P, HP, T], FR)
        KT_hi = sb(scope, "KT_hi", [P, HP, 2, T], FR)
        KT_lo = sb(scope, "KT_lo", [P, HP, 2, T], FR)
        SC = sb(scope, "SC", [P, SG, SD])
        SE = sb(scope, "SE", [P, SG, SD])
        smax = sb(scope, "smax", [P, SG])
        sdiag = sb(scope, "sdiag", [P, SG])
        ssum = sb(scope, "ssum", [P, SG])
        attn = sb(scope, "attn", [P, HH, TT])
        vd = sb(scope, "vd", [P, TT, HH * SD])
        vT_hi = sb(scope, "vT_hi", [P, HP, T], FR)
        vT_lo = sb(scope, "vT_lo", [P, HP, T], FR)
        scope.close()

        S_BANKS = HH * TT // 2
        USES = 2 * HP + S_BANKS + TT + HP
        HIS = 3 * HP

        with nc.Block() as block:

            @block.sync
            def _(sp):
                wp = Wproj.rearrange("(j r) n -> r j n", r=64)
                for twice in range(2):
                    for h in range(2):
                        r0 = 64 * twice + HD * h
                        sp.dma_start(oR[r0:r0 + HD, :, :], r_dram[h].partition_broadcast(HD)) \
                            .then_inc(sem("oR_in"), 16)
                for j0 in range(0, NP, 4):
                    sp.dma_start(oT[:, j0:j0 + 4, :], o_dram[j0:j0 + 4].rearrange("j p t -> p j t")) \
                        .then_inc(sem(f"oT_in{j0}"), 16)
                    for twice in range(2):
                        sp.dma_start(Wp_raw[64 * twice:64 * twice + 64, j0:j0 + 4, :], wp[:, j0:j0 + 4, :]) \
                            .then_inc(sem(f"wp_in{j0}"), 16)
                sp.dma_start(x_sum[:, :, :], x_rows).then_inc(sem("x_again"), 16)
                sp.dma_start(bpr[:, :], bproj.partition_broadcast(P)).then_inc(sem("bp_in"), 16)
                sp.wait_ge(sem("bv_zeroed"), 1)
                sp.dma_start(bvc[0:64, :], bkv[D:2 * D].rearrange("(j r) -> r j", r=64),
                             allow_slow_non_contiguous=True).then_inc(sem("bv_in"), 16)

                sp.wait_ge(sem("proj_made"), TT)
                for half in range(2):
                    heads = slice(HH * half, HH * half + HH)
                    for kind, W in enumerate((WQ, WK, WVd, WVu)):
                        w = 4 * half + kind
                        if w >= 2:
                            sp.wait_ge(sem("sw_lo"), w - 1)
                        if kind < 3:
                            for k in range(KC):
                                sp.dma_start(W2_raw[:, w % 2, k, :].rearrange("p (n d) -> p n d", d=SD),
                                             W[heads, k * P:(k + 1) * P, :].rearrange("n p d -> p n d")) \
                                    .then_inc(sem(f"sw_in{w % 2}"), 16)
                        else:
                            rows = W[heads].rearrange("n d e -> (n d) e")
                            for k in range(KC):
                                sp.dma_start(W2_raw[:, w % 2, k, :], rows[k * P:(k + 1) * P, :]) \
                                    .then_inc(sem(f"sw_in{w % 2}"), 16)

            @block.gpsimd
            def _(pool):
                nc.gpsimd.memset(bvc[:, :], 0.0).then_inc(sem("bv_zeroed"), 1)
                nc.gpsimd.memset(triu[:, :, :], 1.0).then_inc(sem("masks_set"), 1)
                nc.gpsimd.memset(diag[:, :], 0.0).then_inc(sem("masks_set"), 1)
                pool.wait_ge(sem("masks_set"), 2)
                for h in range(2):
                    rows = slice(64 * h, 64 * h + 64)
                    nc.gpsimd.affine_select(out=triu[rows, :, :], in_=triu[rows, :, :], compare_op=ALU.is_ge, fill=0.0,
                                            base=0, pattern=[[0, 2], [1, SD]], channel_multiplier=-1) \
                        .then_inc(sem("masks_ready"), 1)
                    nc.gpsimd.affine_select(out=diag[rows, :], in_=diag[rows, :], compare_op=ALU.not_equal, fill=1.0,
                                            base=0, pattern=[[1, SD]], channel_multiplier=-1) \
                        .then_inc(sem("masks_ready"), 1)
                pool.wait_ge(sem("proj_made"), TT)
                for h in range(2):
                    rows = slice(64 * h, 64 * h + 64)
                    nc.gpsimd.memset(f32(KT_hi[rows, :, 1 - h, :]), 0.0).then_inc(sem("kt_zeroed"), 1)
                    nc.gpsimd.memset(f32(KT_lo[rows, :, 1 - h, :]), 0.0).then_inc(sem("kt_zeroed"), 1)

            @block.scalar
            def _(act):
                for j0 in range(0, NP, 4):
                    act.wait_ge(sem(f"wp_in{j0}"), 32)
                    nc.scalar.copy(Wp_hi[:, j0:j0 + 4, :], Wp_raw[:, j0:j0 + 4, :]).then_inc(sem("wp_hi"), 1)
                for j in range(NP):
                    act.wait_ge(sem("bv_added"), j + 1)
                    nc.scalar.copy(oT_hi[:, j, :], oT[:, j, :]).then_inc(sem("oT_hi"), 1)
                norm_scalar(act, 2, lnt2)
                turn_scalar(act, 2, x2T_hi)

                def split_hi(w):
                    act.wait_ge(sem(f"sw_in{w % 2}"), 64 * (w // 2 + 1))
                    if w >= 2:
                        half, kind = (w - 2) // 4, (w - 2) % 4
                        if kind == 3:
                            act.wait_ge(sem("up_half"), 1)
                        else:
                            act.wait_ge(sem("b_made"), USES * half + (HP, 2 * HP, 2 * HP + S_BANKS + TT)[kind])
                    nc.scalar.copy(W2_hi[:, w % 2, :, :], W2_raw[:, w % 2, :, :]).then_inc(sem("sw_hi"), 1)

                act.wait_ge(sem("kt_zeroed"), 4)
                split_hi(0)
                split_hi(1)
                for half in range(2):
                    use = USES * half
                    for j in range(HP):
                        act.wait_ge(sem("b_made"), use + 1)
                        nc.scalar.copy(QT_hi[:, j, :], bank(4 + use % 4)).then_inc(sem("b_hi"), 1)
                        use += 1
                    split_hi(4 * half + 2)
                    for j in range(HP):
                        act.wait_ge(sem("b_made"), use + 1)
                        for h in range(2):
                            rows = slice(64 * h, 64 * h + 64)
                            ins = nc.scalar.copy(KT_hi[rows, j, h, :], bank(4 + use % 4)[rows, :])
                        ins.then_inc(sem("b_hi"), 1)
                        use += 1
                    split_hi(4 * half + 3)
                    act.wait_ge(sem("s_shifted"), half + 1)
                    nc.scalar.activation(SE[:, :, :], SE[:, :, :], ACT.Exp).then_inc(sem("s_exp"), 1)
                    nc.scalar.activation(sdiag[:, :], sdiag[:, :], ACT.Exp).then_inc(sem("s_exp"), 1)
                    if half == 0:
                        split_hi(4)
                    use = USES * half + 2 * HP + S_BANKS + TT
                    for j in range(HP):
                        act.wait_ge(sem("b_made"), use + 1)
                        nc.scalar.copy(vT_hi[:, j, :], bank(4 + use % 4)).then_inc(sem("b_hi"), 1)
                        use += 1
                    if half == 0:
                        split_hi(5)

            @block.vector
            def _(dve):
                dve.wait_ge(sem("oR_in"), 64)
                for j in range(NP):
                    if j % 4 == 0:
                        dve.wait_ge(sem(f"oT_in{j}"), 16)
                    nc.vector.tensor_tensor(oT[:, j, :], oT[:, j, :], oR[:, j, :], ALU.mult).then_inc(sem("o_normed"), 1)
                dve.wait_ge(sem("bv_in"), 16)
                for j in range(NP):
                    dve.wait_ge(sem("o_normed"), j + 1)
                    nc.vector.tensor_scalar(oT[:, j, :], oT[:, j, :], bvc[:, j:j + 1], None, ALU.add) \
                        .then_inc(sem("bv_added"), 1)
                for j0 in range(0, NP, 4):
                    dve.wait_ge(sem("wp_hi"), j0 // 4 + 1)
                    nc.vector.tensor_tensor(Wp_lo[:, j0:j0 + 4, :], Wp_raw[:, j0:j0 + 4, :],
                                            f32(Wp_hi[:, j0:j0 + 4, :]), ALU.subtract).then_inc(sem("wp_lo"), 1)
                    for j in range(j0, j0 + 4):
                        dve.wait_ge(sem("oT_hi"), j + 1)
                        nc.vector.tensor_tensor(oT_lo[:, j, :], oT[:, j, :], f32(oT_hi[:, j, :]), ALU.subtract) \
                            .then_inc(sem("oT_lo"), 1)
                dve.wait_ge(sem("x_again"), 16)
                dve.wait_ge(sem("bp_in"), 16)
                nc.vector.tensor_tensor(x_sum[:, :, :], x_sum[:, :, :],
                                        bpr[:, :].unsqueeze(1).broadcast_to([P, TT, D]), ALU.add) \
                    .then_inc(sem("x_base"), 1)
                dve.wait_ge(sem("x_base"), 1)
                for t in range(TT):
                    dve.wait_ge(sem("proj_made"), t + 1)
                    nc.vector.tensor_tensor(x_sum[:, t, :], x_sum[:, t, :], bank(t), ALU.add).then_inc(sem("x_1"), 1)
                dve.wait_ge(sem("x_1"), TT)
                norm_vector(dve, 2, x_sum, xn2, lnt2)
                turn_vector(dve, 2, x2T_hi, x2T_lo)
                dve.wait_ge(sem("ln_done"), 2)
                nc.vector.tensor_tensor(x_sum[:, :, :], x_sum[:, :, :], xn2[:, :, :], ALU.add) \
                    .then_inc(sem("x_1"), 1)

                def split_lo(w):
                    dve.wait_ge(sem("sw_hi"), w + 1)
                    nc.vector.tensor_tensor(W2_lo[:, w % 2, :, :], W2_raw[:, w % 2, :, :],
                                            f32(W2_hi[:, w % 2, :, :]), ALU.subtract).then_inc(sem("sw_lo"), 1)

                step = [0]

                def link(ins):
                    step[0] += 1
                    ins.then_inc(sem("soft_step"), 1)
                    dve.wait_ge(sem("soft_step"), step[0])

                split_lo(0)
                split_lo(1)
                dve.wait_ge(sem("masks_ready"), 4)
                for half in range(2):
                    use, his = USES * half, HIS * half
                    for j in range(HP):
                        dve.wait_ge(sem("b_hi"), his + 1)
                        nc.vector.tensor_tensor(QT_lo[:, j, :], bank(4 + use % 4), f32(QT_hi[:, j, :]), ALU.subtract) \
                            .then_inc(sem("b_done"), 1)
                        use += 1
                        his += 1
                    split_lo(4 * half + 2)
                    for j in range(HP):
                        dve.wait_ge(sem("b_hi"), his + 1)
                        for h in range(2):
                            rows = slice(64 * h, 64 * h + 64)
                            ins = nc.vector.tensor_tensor(KT_lo[rows, j, h, :], bank(4 + use % 4)[rows, :],
                                                          f32(KT_hi[rows, j, h, :]), ALU.subtract)
                        ins.then_inc(sem("b_done"), 1)
                        use += 1
                        his += 1
                    split_lo(4 * half + 3)
                    for n in range(HH):
                        for w in range(TT // 2):
                            dve.wait_ge(sem("b_made"), use + 1)
                            blocks = bank(4 + use % 4).rearrange("p (a c) -> p a c", c=2 * SD)
                            for h in range(2):
                                rows = slice(64 * h, 64 * h + 64)
                                g0 = n * TT + 2 * w
                                ins = nc.vector.scalar_tensor_tensor(
                                    out=SC[rows, g0:g0 + 2, :], in0=blocks[rows, 0:4:3, 64 * h:64 * h + 64],
                                    scalar=SD ** -0.5, in1=triu[rows, :, :], op0=ALU.mult, op1=ALU.mult)
                            ins.then_inc(sem("b_done"), 1)
                            use += 1
                    dve.wait_ge(sem("b_done"), use)
                    link(nc.vector.tensor_scalar(SE[:, :, :], SC[:, :, :], 0.0, FMIN, ALU.is_equal, ALU.mult))
                    link(nc.vector.tensor_tensor(SC[:, :, :], SC[:, :, :], SE[:, :, :], ALU.add))
                    link(nc.vector.tensor_tensor(SE[:, :, :], SC[:, :, :],
                                                 diag[:, :].unsqueeze(1).broadcast_to([P, SG, SD]), ALU.mult))
                    link(nc.vector.tensor_reduce(sdiag[:, :], SE[:, :, :], AX.X, ALU.add))
                    link(nc.vector.tensor_reduce(smax[:, :], SC[:, :, :], AX.X, ALU.max))
                    link(nc.vector.tensor_tensor(sdiag[:, :], sdiag[:, :], smax[:, :], ALU.subtract))
                    nc.vector.tensor_tensor(SE[:, :, :], SC[:, :, :],
                                            smax[:, :].unsqueeze(2).broadcast_to([P, SG, SD]), ALU.subtract) \
                        .then_inc(sem("s_shifted"), 1)
                    dve.wait_ge(sem("s_exp"), 2 * half + 2)
                    link(nc.vector.tensor_reduce(ssum[:, :], SE[:, :, :], AX.X, ALU.add))
                    link(nc.vector.reciprocal(ssum[:, :], ssum[:, :]))
                    link(nc.vector.scalar_tensor_tensor(out=attn[:, :, :].rearrange("p n t -> p (n t)"),
                                                        in0=sdiag[:, :], scalar=1.0 / SH, in1=ssum[:, :],
                                                        op0=ALU.mult, op1=ALU.mult))
                    for t in range(TT):
                        dve.wait_ge(sem("b_made"), use + 1)
                        nc.vector.tensor_tensor(vd[:, t, :].rearrange("p (n d) -> p n d", d=SD),
                                                bank(4 + use % 4).rearrange("p (n d) -> p n d", d=SD),
                                                attn[:, :, t:t + 1].broadcast_to([P, HH, SD]), ALU.mult) \
                            .then_inc(sem("b_done"), 1)
                        use += 1
                    if half == 0:
                        split_lo(4)
                    for j in range(HP):
                        dve.wait_ge(sem("b_hi"), his + 1)
                        nc.vector.tensor_tensor(vT_lo[:, j, :], bank(4 + use % 4), f32(vT_hi[:, j, :]), ALU.subtract) \
                            .then_inc(sem("b_done"), 1)
                        use += 1
                        his += 1
                    if half == 0:
                        split_lo(5)
                dve.wait_ge(sem("x_1"), TT + 1)
                for t in range(TT):
                    dve.wait_ge(sem("up_made"), t + 1)
                    nc.vector.tensor_tensor(x_sum[:, t, :], x_sum[:, t, :], bank(t), ALU.add).then_inc(sem("x_2"), 1)

            @block.tensor
            def _(pe):
                for t in range(TT):
                    cols = slice(t * P, (t + 1) * P)
                    for j in range(NP):
                        if t == 0:
                            pe.wait_ge(sem("wp_lo"), j // 4 + 1)
                            pe.wait_ge(sem("oT_lo"), j + 1)
                        nc.tensor.matmul(bank(t), oT_hi[:, j, cols], Wp_hi[:, j, :], start=(j == 0), stop=False)
                        nc.tensor.matmul(bank(t), oT_hi[:, j, cols], Wp_lo[:, j, :], start=False, stop=False)
                        ins = nc.tensor.matmul(bank(t), oT_lo[:, j, cols], Wp_hi[:, j, :], start=False,
                                               stop=(j == NP - 1))
                    ins.then_inc(sem("proj_made"), 1)
                turn_tensor(pe, 2, xn2)
                pe.wait_ge(sem("x_turned_lo"), 2 * KC)

                def take(use):
                    if use >= 4:
                        pe.wait_ge(sem("b_done"), use - 3)
                    return bank(4 + use % 4)

                for half in range(2):
                    use = USES * half

                    def columns(w):
                        nonlocal use
                        pe.wait_ge(sem("sw_lo"), w + 1)
                        for j in range(HP):
                            cols = slice(j * P, (j + 1) * P)
                            ins = three(pe, take(use), [((W2_hi[:, w % 2, k, cols], W2_lo[:, w % 2, k, cols]),
                                                         (x2T_hi[:, k, :], x2T_lo[:, k, :])) for k in range(KC)])
                            ins.then_inc(sem("b_made"), 1)
                            use += 1
                        return ins

                    columns(4 * half)
                    columns(4 * half + 1)
                    pe.wait_ge(sem("b_done"), use)
                    for n in range(HH):
                        j, h = n // 2, n % 2
                        for w in range(TT // 2):
                            out_bank = take(use)
                            for r in range(2):
                                g = 2 * w + r
                                keys = slice(g * P, (g + 1) * P)
                                window = slice(2 * w * P, 2 * (w + 1) * P)
                                ins = three(pe, out_bank[:, 2 * P * r:2 * P * (r + 1)],
                                            [((KT_hi[:, j, h, keys], KT_lo[:, j, h, keys]),
                                              (QT_hi[:, j, window], QT_lo[:, j, window]))])
                            ins.then_inc(sem("b_made"), 1)
                            use += 1
                    w = 4 * half + 2
                    pe.wait_ge(sem("sw_lo"), w + 1)
                    for t in range(TT):
                        cols = slice(t * P, (t + 1) * P)
                        three(pe, take(use), [((x2T_hi[:, k, cols], x2T_lo[:, k, cols]),
                                               (W2_hi[:, w % 2, k, :], W2_lo[:, w % 2, k, :])) for k in range(KC)]) \
                            .then_inc(sem("b_made"), 1)
                        use += 1
                    pe.wait_ge(sem("b_done"), use)
                    for j in range(HP):
                        b_out = take(use)
                        for t in range(TT):
                            ins = nc.tensor.matmul(b_out[:, t * P:(t + 1) * P], vd[:, t, j * P:(j + 1) * P],
                                                   ident[:, :], is_transpose=True, start=True, stop=True)
                        ins.then_inc(sem("b_made"), 1)
                        use += 1
                    w = 4 * half + 3
                    pe.wait_ge(sem("sw_lo"), w + 1)
                    pe.wait_ge(sem("b_done"), use)
                    for t in range(TT):
                        cols = slice(t * P, (t + 1) * P)
                        for j in range(HP):
                            first, last = half == 0 and j == 0, half == 1 and j == HP - 1
                            nc.tensor.matmul(bank(t), vT_hi[:, j, cols], W2_hi[:, w % 2, j, :], start=first, stop=False)
                            nc.tensor.matmul(bank(t), vT_hi[:, j, cols], W2_lo[:, w % 2, j, :], start=False, stop=False)
                            ins = nc.tensor.matmul(bank(t), vT_lo[:, j, cols], W2_hi[:, w % 2, j, :],
                                                   start=False, stop=last)
                        if half == 1:
                            ins.then_inc(sem("up_made"), 1)
                        elif t == TT - 1:
                            ins.then_inc(sem("up_half"), 1)

        NE, _, H = W1.shape
        TOP = 2
        QT = H // 512
        HC = H // P
        TILES = NE + (TOP * T) // (P + 1)
        ROWS = TILES + 1
        FAR = 10000.0
        GATE_EPS = 1e-12
        UNITS = 2 * QT
        UNIT_ORDER = [("1", 0), ("1", 1), ("1", 2), ("2", 0), ("1", 3), ("2", 1), ("2", 2), ("2", 3)]
        UNIT_OF = {u: n for n, u in enumerate(UNIT_ORDER)}
        assert len(UNIT_ORDER) == UNITS and QT == 4 and D == 512

        scope = ExitStack()
        wu_hi = sb(scope, "wu_hi", [P, UNITS, 4, D], FR)
        xg_hi = sb(scope, "xg_hi", [P, TT, D], FR)
        xg_lo = sb(scope, "xg_lo", [P, TT, D], FR)
        b1rows = sb(scope, "b1rows", [P, H], FR)
        iota_s = sb(scope, "iota_s", [P, P])
        ones_r = sb(scope, "ones_r", [P, P], FR)
        table = sb(scope, "table", [P, ROWS, 2, TT])
        first_i = sb(scope, "first_i", [P, NE], I32)
        last_i = sb(scope, "last_i", [P, NE], I32)
        cur = sb(scope, "cur", [P, 2, TT])
        gate2 = sb(scope, "gate2", [P, TT, 2], FR)
        gs = sb(scope, "gs", [P, 1])
        gating = ExitStack()
        lnt3 = (sb(gating, "st3", [P, TT, 6]), sb(gating, "mv3", [P, TT, 2]), sb(gating, "ve3", [P, TT]),
                sb(gating, "rt3", [P, TT]), sb(gating, "rs3", [P, TT]))
        xn3 = sb(gating, "xn3", [P, TT, D])
        x3T_hi = sb(gating, "x3T_hi", [P, KC, T], FR)
        x3T_lo = sb(gating, "x3T_lo", [P, KC, T], FR)
        Wg_raw = sb(gating, "Wg_raw", [P, KC, NE])
        Wg_hi = sb(gating, "Wg_hi", [P, KC, NE], FR)
        Wg_lo = sb(gating, "Wg_lo", [P, KC, NE], FR)
        bgr = sb(gating, "bgr", [P, NE])
        b1_raw = sb(gating, "b1_raw", [P, P])
        b1_hi = sb(gating, "b1_hi", [P, P], FR)
        b1_lo = sb(gating, "b1_lo", [P, P], FR)
        b2_sb = sb(gating, "b2_sb", [NE, D])
        gT = sb(gating, "gT", [NE, T])
        before = sb(gating, "before", [P, P], BF16)
        ones = sb(gating, "ones", [P, P], BF16)
        iota_e = sb(gating, "iota_e", [P, NE])
        rev_e = sb(gating, "rev_e", [P, TT, NE])
        iota_i = sb(gating, "iota_i", [P, ROWS, NE])
        G3 = [P, TT, NE]
        gate = sb(gating, "gate", G3)
        work = sb(gating, "work", G3)
        key = sb(gating, "key", G3)
        hot1 = sb(gating, "hot1", G3)
        hot2 = sb(gating, "hot2", G3)
        rank = sb(gating, "rank", G3)
        chosen = sb(gating, "chosen", G3, BF16)
        col = sb(gating, "col", [P, TT])
        cnt = sb(gating, "cnt", [P, NE])
        more = sb(gating, "more", [P, NE])
        start_at = sb(gating, "start_at", [P, NE + 1])
        I3 = [P, ROWS, NE]
        in_e = sb(gating, "in_e", I3)
        tmp_i = sb(gating, "tmp_i", I3)
        base = sb(gating, "base", [P, ROWS])
        gating.close()
        sel = sb(scope, "sel", [P, TT, P], FR)
        selT = sb(scope, "selT", [P, T], FR)
        gathered = sb(scope, "gathered", [P, D])
        gT_hi = sb(scope, "gT_hi", [P, KC, P], FR)
        gT_lo = sb(scope, "gT_lo", [P, KC, P], FR)
        hid = sb(scope, "hid", [P, 2, 512])
        h_hi = sb(scope, "h_hi", [P, 2, 4, P], FR)
        h_lo = sb(scope, "h_lo", [P, 2, 4, P], FR)
        eo_hi = sb(scope, "eo_hi", [P, D], FR)
        eo_lo = sb(scope, "eo_lo", [P, D], FR)
        arrival = ExitStack()
        wu_raw_back = sb(arrival, "wu_raw", [P, UNITS, 4, D])
        arrival.close()
        wu_lo_back = sb(scope, "wu_lo", [P, UNITS, 4, D], FR)
        EARLY_UNITS = 6
        scope.close()

        def wu_raw(v):
            return wu_raw_back[:, UNITS - 1 - v, :, :]

        def wu_lo(v):
            return wu_lo_back[:, UNITS - 1 - v, :, :]

        b1_dram = nc.dram_tensor("b1_parts", [2, NE * H], F32, kind="Internal").ap()

        EO_CREDIT = 1

        def load_tile(eng, tiles, e):
            return eng.value_load(tiles[0:1, bass.ds(e, 1)], min_val=0, max_val=TILES - 1)

        def for_tiles(eng, body):
            with eng.Fori(0, NE - 1) as e:
                first, last = load_tile(eng, first_i, e), load_tile(eng, last_i, e)
                with eng.If(first < last):
                    with eng.Fori(first, last) as t:
                        body(e, t, False)
                body(e, last, True)
            first, last = load_tile(eng, first_i, NE - 1), load_tile(eng, last_i, NE - 1)
            with eng.Fori(first, last + 1) as t:
                body(NE - 1, t, False)

        with nc.Block() as block:

            @block.sync
            def _(sp):
                sp.dma_start(Wg_raw[:, :, :], Wg.rearrange("(k p) e -> p k e", p=P)).then_inc(sem("wg_in"), 16)
                sp.dma_start(bgr[:, :], bg.partition_broadcast(P)).then_inc(sem("bg_in"), 16)
                sp.dma_start(b1_raw[:, :], b1.rearrange("e (c p) -> (e c) p", p=P)).then_inc(sem("b1_in"), 16)
                sp.dma_start(b2_sb[:, :], b2).then_inc(sem("b2_in"), 16)

                def load_unit(e, v):
                    which, q = UNIT_ORDER[v]
                    W = (W1 if which == "1" else W2)[bass.ds(e, 1)].rearrange("a r c -> (a r) c")
                    src = W[:, q * 512:(q + 1) * 512] if which == "1" else W[q * 512:(q + 1) * 512, :]
                    sp.dma_start(wu_raw(v), src.rearrange("(k p) c -> p k c", p=P)).then_inc(sem(f"wu_in{v}"), 16)

                def load_b1(e):
                    sp.dma_start(f32(b1rows[0:2, :]), b1_dram[:, bass.ds(e * H, H)]).then_inc(sem("b1row_in"), 16)

                for v in range(EARLY_UNITS):
                    load_unit(0, v)
                sp.wait_ge(sem("b1_split"), 1)
                for part, b1_part in enumerate((b1_hi, b1_lo)):
                    sp.dma_start(b1_dram[part].rearrange("(r c) -> r c", c=P), f32(b1_part[:, :])) \
                        .then_inc(sem("b1_out"), 16)
                sp.wait_ge(sem("b1_out"), 32)
                sp.wait_ge(sem("b1rows_zeroed"), 1)
                load_b1(0)
                sp.wait_ge(sem("table_ready"), 1)
                for v in range(EARLY_UNITS, UNITS):
                    load_unit(0, v)

                def tile(e, t, change):
                    if not change:
                        return
                    for v, (which, q) in enumerate(UNIT_ORDER):
                        sp.wait_ge(sem(f"l{which}_made"), t * QT + q + 1)
                        load_unit(e + 1, v)
                        if (which, q) == ("1", 3):
                            load_b1(e + 1)

                with sp.Fori(0, NE - 1) as e:
                    tile(e, load_tile(sp, last_i, e), True)
                for t in range(TT):
                    sp.wait_ge(sem("x_3"), t + 1)
                    sp.dma_start(out_rows[:, t, :], x_sum[:, t, :]).then_inc(sem("stored"), 16)
                sp.wait_ge(sem("stored"), 16 * TT)

            @block.gpsimd
            def _(pool):
                nc.gpsimd.memset(f32(b1rows[:, :]), 0.0).then_inc(sem("b1rows_zeroed"), 1)
                nc.gpsimd.memset(before[:, :], 1.0).then_inc(sem("masks_set"), 1)
                nc.gpsimd.memset(ones[:, :], 1.0).then_inc(sem("masks_set"), 1)
                pool.wait_ge(sem("masks_set"), 4)
                nc.gpsimd.affine_select(out=before[:, :], in_=before[:, :], compare_op=ALU.is_gt, fill=0.0, base=0,
                                        pattern=[[1, P]], channel_multiplier=-1).then_inc(sem("c_ready"), 1)
                for t, pattern, at in ((iota_s, [[1, P]], 0), (iota_e, [[1, NE]], 0),
                                       (rev_e, [[0, TT], [-1, NE]], NE), (iota_i, [[1, ROWS], [0, NE]], 0)):
                    nc.gpsimd.iota(t[tuple(slice(None) for _ in t.shape)], pattern, base=at, channel_multiplier=0,
                                   allow_small_or_imprecise_dtypes=True).then_inc(sem("c_ready"), 1)

            @block.scalar
            def _(act):
                def first_hi(v):
                    act.wait_ge(sem(f"wu_in{v}"), 16)
                    nc.scalar.copy(wu_hi[:, v, :, :], wu_raw(v)).then_inc(sem("wu_hi_done"), 1)

                norm_scalar(act, 3, lnt3)
                act.wait_ge(sem("ln_done"), 3)
                nc.scalar.copy(xg_hi[:, :, :], xn3[:, :, :]).then_inc(sem("xg_hi"), 1)
                act.wait_ge(sem("wg_in"), 16)
                nc.scalar.copy(Wg_hi[:, :, :], Wg_raw[:, :, :]).then_inc(sem("wg_hi"), 1)
                nc.scalar.copy(ident_r[:, :], ident[:, :]).then_inc(sem("ident_r"), 1)
                turn_scalar(act, 3, x3T_hi)
                act.wait_ge(sem("b1_in"), 16)
                nc.scalar.copy(b1_hi[:, :], b1_raw[:, :]).then_inc(sem("b1_hi"), 1)
                nc.scalar.activation(ones_r[:, :], ident[:, :], ACT.Copy, bias=1.0, scale=0.0).then_inc(sem("ones_r"), 1)
                first_hi(0)
                first_hi(1)
                act.wait_ge(sem("g_shifted"), 1)
                nc.scalar.activation(gate[:, :, :], gate[:, :, :], ACT.Exp).then_inc(sem("g_exp"), 1)

                for v in range(2, EARLY_UNITS):
                    first_hi(v)
                act.wait_ge(sem("table_ready"), 1)
                nc.scalar.activation(selT[:, :], x_sum[:, 0, :], ACT.Copy, scale=0.0)
                nc.scalar.activation(eo_hi[:, :], x_sum[:, 0, :], ACT.Copy, scale=0.0).then_inc(sem("eo_zeroed"), 1)
                act.wait_ge(sem("g_made"), 1)
                nc.scalar.copy(gathered[:, :], bank(4)).then_inc(sem("g_copied"), 1)
                act.wait_ge(sem("g_turned"), 1)
                nc.scalar.copy(gT_hi[:, :, :], bank(6).rearrange("p (k s) -> p k s", s=P)).then_inc(sem("g_hi"), 1)
                for v in range(EARLY_UNITS, UNITS):
                    first_hi(v)

                def tile(e, t, change):
                    def unit_hi(v):
                        if not change:
                            return
                        act.wait_ge(sem(f"wu_in{v}"), (e + 2) * 16)
                        nc.scalar.copy(wu_hi[:, v, :, :], wu_raw(v)) \
                            .then_inc(sem("wu_hi_done"), 1)

                    def gelu(q):
                        act.wait_ge(sem("l1_made"), t * QT + q + 1)
                        if q >= 2:
                            act.wait_ge(sem("h_turned"), t * QT + q - 1)
                        nc.scalar.activation(hid[:, q % 2, :], bank(4 + q % 2), ACT.Gelu).then_inc(sem("h_made"), 1)

                    def hidden_hi(q):
                        act.wait_ge(sem("h_turned"), t * QT + q + 1)
                        if q >= 2:
                            act.wait_ge(sem("l2_made"), t * QT + q - 1)
                        nc.scalar.copy(h_hi[:, q % 2, :, :], bank(6).rearrange("p (c s) -> p c s", s=P)) \
                            .then_inc(sem("h_hi"), 1)

                    gelu(0)
                    act.wait_ge(sem("selT_made"), t + 1)
                    nc.scalar.copy(selT[:, :], bank(6)).then_inc(sem("selT_done"), 1)
                    gelu(1)
                    hidden_hi(0)
                    unit_hi(0)
                    unit_hi(1)
                    gelu(2)
                    hidden_hi(1)
                    unit_hi(2)
                    unit_hi(3)
                    gelu(3)
                    hidden_hi(2)
                    unit_hi(4)
                    act.wait_ge(sem("g_made"), t + 2)
                    nc.scalar.copy(gathered[:, :], bank(4)).then_inc(sem("g_copied"), 1)
                    hidden_hi(3)
                    unit_hi(5)
                    act.wait_ge(sem("g_turned"), t + 2)
                    nc.scalar.copy(gT_hi[:, :, :], bank(6).rearrange("p (k s) -> p k s", s=P)) \
                        .then_inc(sem("g_hi"), 1)
                    unit_hi(6)
                    unit_hi(7)

                for_tiles(act, tile)

            @block.vector
            def _(dve):
                norm_vector(dve, 3, x_sum, xn3, lnt3)
                dve.wait_ge(sem("xg_hi"), 1)
                nc.vector.tensor_tensor(xg_lo[:, :, :], xn3[:, :, :], f32(xg_hi[:, :, :]), ALU.subtract) \
                    .then_inc(sem("xg_lo"), 1)
                dve.wait_ge(sem("wg_hi"), 1)
                nc.vector.tensor_tensor(Wg_lo[:, :, :], Wg_raw[:, :, :], f32(Wg_hi[:, :, :]), ALU.subtract) \
                    .then_inc(sem("wg_lo"), 1)
                turn_vector(dve, 3, x3T_hi, x3T_lo)

                def first_lo(v):
                    dve.wait_ge(sem("wu_hi_done"), v + 1)
                    nc.vector.tensor_tensor(wu_lo(v), wu_raw(v), f32(wu_hi[:, v, :, :]),
                                            ALU.subtract).then_inc(sem("wu_lo_done"), 1)

                dve.wait_ge(sem("b1_hi"), 1)
                nc.vector.tensor_tensor(b1_lo[:, :], b1_raw[:, :], f32(b1_hi[:, :]), ALU.subtract) \
                    .then_inc(sem("b1_split"), 1)

                step = [0]

                def link(ins):
                    step[0] += 1
                    ins.then_inc(sem("gate_step"), 1)
                    dve.wait_ge(sem("gate_step"), step[0])

                tt, ts, red = nc.vector.tensor_tensor, nc.vector.tensor_scalar, nc.vector.tensor_reduce

                def over_e(c):
                    return c[:, :].unsqueeze(2).broadcast_to([P, TT, NE])

                dve.wait_ge(sem("bg_in"), 16)
                dve.wait_ge(sem("logits_made"), 1)
                link(tt(gate[:, :, :], bank(4)[:, 0:TT * NE].rearrange("p (t e) -> p t e", e=NE),
                        bgr[:, :].unsqueeze(1).broadcast_to([P, TT, NE]), ALU.add))
                link(red(col[:, :], gate[:, :, :], AX.X, ALU.max))
                tt(gate[:, :, :], gate[:, :, :], over_e(col), ALU.subtract).then_inc(sem("g_shifted"), 1)
                dve.wait_ge(sem("g_exp"), 1)
                link(red(col[:, :], gate[:, :, :], AX.X, ALU.add))
                link(nc.vector.reciprocal(col[:, :], col[:, :]))
                link(tt(gate[:, :, :], gate[:, :, :], over_e(col), ALU.mult))
                first_lo(0)
                dve.wait_ge(sem("c_ready"), 5)
                link(nc.vector.tensor_copy(work[:, :, :], gate[:, :, :]))
                for hot in (hot1, hot2):
                    link(red(col[:, :], work[:, :, :], AX.X, ALU.max))
                    link(tt(key[:, :, :], work[:, :, :], over_e(col), ALU.is_equal))
                    link(tt(key[:, :, :], key[:, :, :], rev_e[:, :, :], ALU.mult))
                    link(red(col[:, :], key[:, :, :], AX.X, ALU.max))
                    link(tt(hot[:, :, :], key[:, :, :], over_e(col), ALU.is_equal))
                    if hot is hot1:
                        link(nc.vector.scalar_tensor_tensor(
                            out=work[:, :, :].rearrange("p t e -> p (t e)"),
                            in0=hot[:, :, :].rearrange("p t e -> p (t e)"), scalar=-2.0,
                            in1=work[:, :, :].rearrange("p t e -> p (t e)"), op0=ALU.mult, op1=ALU.add))
                link(tt(hot1[:, :, :], hot1[:, :, :], hot2[:, :, :], ALU.add))
                nc.vector.tensor_copy(chosen[:, :, :], hot1[:, :, :]).then_inc(sem("chosen_ready"), 1)
                link(tt(gate[:, :, :], gate[:, :, :], hot1[:, :, :], ALU.mult))
                link(red(col[:, :], gate[:, :, :], AX.X, ALU.add))
                link(ts(col[:, :], col[:, :], GATE_EPS, None, ALU.max))
                link(nc.vector.reciprocal(col[:, :], col[:, :]))
                tt(gate[:, :, :], gate[:, :, :], over_e(col), ALU.mult).then_inc(sem("gates_ready"), 1)
                dve.wait_ge(sem("gates_ready"), 1)

                first_lo(1)
                dve.wait_ge(sem("ranks_made"), 1)
                link(ts(rank[:, :, :], bank(5)[:, 0:TT * NE].rearrange("p (t e) -> p t e", e=NE), FAR, None, ALU.add))
                link(tt(rank[:, :, :], rank[:, :, :], hot1[:, :, :], ALU.mult))
                link(ts(rank[:, :, :], rank[:, :, :], FAR, None, ALU.subtract))
                link(ts(cnt[:, :], bank(5)[:, TT * NE:(TT + 1) * NE], float(P), 1.0, ALU.is_gt, ALU.add))
                for full in range(2, T // P):
                    link(ts(more[:, :], bank(5)[:, TT * NE:(TT + 1) * NE], float(full * P), None, ALU.is_gt))
                    link(tt(cnt[:, :], cnt[:, :], more[:, :], ALU.add))
                link(nc.vector.memset(start_at[:, 0:1], 0.0))
                for e in range(NE):
                    link(tt(start_at[:, e + 1:e + 2], start_at[:, e:e + 1], cnt[:, e:e + 1], ALU.add))
                link(nc.vector.tensor_copy(first_i[:, :], start_at[:, 0:NE]))
                link(ts(last_i[:, :], start_at[:, 1:NE + 1], 1.0, None, ALU.subtract))
                link(tt(in_e[:, :, :], iota_i[:, :, :],
                        start_at[:, 0:NE].unsqueeze(1).broadcast_to([P, ROWS, NE]), ALU.is_ge))
                link(tt(tmp_i[:, :, :], iota_i[:, :, :],
                        start_at[:, 1:NE + 1].unsqueeze(1).broadcast_to([P, ROWS, NE]), ALU.is_lt))
                link(tt(in_e[:, :, :], in_e[:, :, :], tmp_i[:, :, :], ALU.mult))
                link(tt(tmp_i[:, :, :], iota_i[:, :, :],
                        start_at[:, 0:NE].unsqueeze(1).broadcast_to([P, ROWS, NE]), ALU.subtract))
                link(tt(tmp_i[:, :, :], tmp_i[:, :, :], in_e[:, :, :], ALU.mult))
                link(red(base[:, :], tmp_i[:, :, :], AX.X, ALU.add))
                link(ts(base[:, :], base[:, :], float(P), None, ALU.mult))
                for t in range(TT):
                    for n, of in enumerate((rank, gate)):
                        link(tt(tmp_i[:, :, :], in_e[:, :, :], of[:, t, :].unsqueeze(1).broadcast_to([P, ROWS, NE]),
                                ALU.mult))
                        link(red(table[:, :, n, t], tmp_i[:, :, :], AX.X, ALU.add))
                    link(tt(table[:, :, 0, t], table[:, :, 0, t], base[:, :], ALU.subtract))
                dve.wait_ge(sem("gT_turned"), 1)
                nc.vector.tensor_copy(gT[:, :], bank(7)[0:NE, :]).then_inc(sem("gT_ready"), 1)
                dve.wait_ge(sem("y_begun"), 1)
                dve.wait_ge(sem("b1_out"), 32)
                dve.sem_inc(sem("table_ready"), 1)

                at = [0]

                def link_look(ins, t):
                    at[0] += 1
                    ins.then_inc(sem("look_step"), 1)
                    dve.wait_ge(sem("look_step"), t * 2 + 2 - at[0] % 2)

                def look_up(t):
                    link_look(nc.vector.tensor_copy(cur[:, :, :], table[:, bass.ds(t, 1), :, :]
                                               .rearrange("p a n t -> p (a n) t")), t)
                    link_look(nc.vector.tensor_copy(gate2[:, :, 0], cur[:, 1, :]), t)
                    nc.vector.tensor_tensor(gate2[:, :, 1], cur[:, 1, :], f32(gate2[:, :, 0]), ALU.subtract)
                    for n in range(TT):
                        ins = nc.vector.tensor_scalar(sel[:, n, :], iota_s[:, :], cur[:, 0, n:n + 1], None,
                                                      ALU.is_equal)
                    ins.then_inc(sem("sel_ready"), 1)

                def gathered_lo(t):
                    dve.wait_ge(sem("g_hi"), t + 1)
                    nc.vector.tensor_tensor(gT_lo[:, :, :], bank(6).rearrange("p (k s) -> p k s", s=P),
                                            f32(gT_hi[:, :, :]), ALU.subtract).then_inc(sem("g_lo"), 1)

                look_up(0)
                dve.wait_ge(sem("eo_zeroed"), 1)
                nc.vector.tensor_copy(eo_lo[:, :], f32(eo_hi[:, :])).then_inc(sem("eo_split"), EO_CREDIT)
                for v in range(2, EARLY_UNITS):
                    first_lo(v)
                gathered_lo(0)
                for v in range(EARLY_UNITS, UNITS):
                    first_lo(v)

                def tile(e, t, change):
                    def unit_lo(v):
                        if not change:
                            return
                        dve.wait_ge(sem("wu_hi_done"), (e + 1) * UNITS + v + 1)
                        nc.vector.tensor_tensor(wu_lo(v), wu_raw(v), f32(wu_hi[:, v, :, :]),
                                                ALU.subtract).then_inc(sem("wu_lo_done"), 1)

                    def hidden_lo(q):
                        dve.wait_ge(sem("h_hi"), t * QT + q + 1)
                        nc.vector.tensor_tensor(h_lo[:, q % 2, :, :], bank(6).rearrange("p (c s) -> p c s", s=P),
                                                f32(h_hi[:, q % 2, :, :]), ALU.subtract).then_inc(sem("h_lo"), 1)

                    dve.wait_ge(sem("gs_made"), t + 1)
                    nc.vector.tensor_reduce(gs[:, :], bank(7)[:, 0:2], AX.X, ALU.add).then_inc(sem("gs_done"), 1)
                    look_up(t + 1)
                    hidden_lo(0)
                    unit_lo(0)
                    unit_lo(1)
                    hidden_lo(1)
                    unit_lo(2)
                    unit_lo(3)
                    hidden_lo(2)
                    unit_lo(4)
                    hidden_lo(3)
                    gathered_lo(t + 1)
                    unit_lo(5)
                    dve.wait_ge(sem("l2_made"), (t + 1) * QT)
                    nc.vector.tensor_scalar(eo_hi[:, :], bank(7), gs[:, 0:1], None, ALU.mult).then_inc(sem("eo_hi"), 1)
                    dve.wait_ge(sem("eo_hi"), t + 1)
                    nc.vector.scalar_tensor_tensor(out=eo_lo[:, :], in0=bank(7), scalar=gs[:, 0:1],
                                                   in1=f32(eo_hi[:, :]), op0=ALU.mult, op1=ALU.subtract) \
                        .then_inc(sem("eo_split"), 1)
                    unit_lo(6)
                    unit_lo(7)

                for_tiles(dve, tile)
                dve.wait_ge(sem("y_made"), 1)
                for t in range(TT):
                    nc.vector.tensor_tensor(x_sum[:, t, :], x_sum[:, t, :], bank(t), ALU.add).then_inc(sem("x_3"), 1)

            @block.tensor
            def _(pe):
                turn_tensor(pe, 3, xn3)
                pe.wait_ge(sem("x_turned_lo"), 3 * KC)
                pe.wait_ge(sem("wg_lo"), 1)
                for t in range(TT):
                    cols = slice(t * P, (t + 1) * P)
                    ins = three(pe, bank(4)[:, t * NE:(t + 1) * NE],
                                [((x3T_hi[:, k, cols], x3T_lo[:, k, cols]), (Wg_hi[:, k, :], Wg_lo[:, k, :]))
                                 for k in range(KC)])
                ins.then_inc(sem("logits_made"), 1)
                pe.wait_ge(sem("chosen_ready"), 1)
                for t in range(TT):
                    for u in range(t + 1):
                        ins = nc.tensor.matmul(bank(5)[:, t * NE:(t + 1) * NE], (before if u == t else ones)[:, :],
                                               chosen[:, u, :], start=(u == 0), stop=(u == t))
                for u in range(TT):
                    ins = nc.tensor.matmul(bank(5)[:, TT * NE:(TT + 1) * NE], ones[:, :], chosen[:, u, :],
                                           start=(u == 0), stop=(u == TT - 1))
                ins.then_inc(sem("ranks_made"), 1)
                pe.wait_ge(sem("gates_ready"), 1)
                for t in range(TT):
                    ins = nc.tensor.matmul(bank(7)[0:NE, t * P:(t + 1) * P], gate[:, t, :], ident[:, :],
                                           is_transpose=True, start=True, stop=True)
                ins.then_inc(sem("gT_turned"), 1)
                pe.wait_ge(sem("gT_ready"), 1)
                pe.wait_ge(sem("b2_in"), 16)
                for t in range(TT):
                    ins = nc.tensor.matmul(bank(t), gT[:, t * P:(t + 1) * P], b2_sb[:, :], start=True, stop=False,
                                           skip_group_check=True)
                ins.then_inc(sem("y_begun"), 1)
                pe.wait_ge(sem("xg_lo"), 1)
                pe.wait_ge(sem("ident_r"), 1)
                pe.wait_ge(sem("ones_r"), 1)
                pe.wait_ge(sem("b1rows_zeroed"), 1)
                pe.wait_ge(sem("table_ready"), 1)

                def gather(t):
                    pe.wait_ge(sem("sel_ready"), t + 1)
                    for n, (c, part) in enumerate((c, part) for c in range(TT) for part in (xg_hi, xg_lo)):
                        ins = nc.tensor.matmul(bank(4), sel[:, c, :], part[:, c, :],
                                               start=(n == 0), stop=(n == 2 * TT - 1))
                    ins.then_inc(sem("g_made"), 1)

                def turn_gathered(t):
                    pe.wait_ge(sem("g_copied"), t + 1)
                    for k in range(KC):
                        ins = nc.tensor.matmul(bank(6)[:, k * P:(k + 1) * P], gathered[:, k * P:(k + 1) * P],
                                               ident[:, :], is_transpose=True, start=True, stop=True)
                    ins.then_inc(sem("g_turned"), 1)

                def scatter(done):
                    pe.wait_ge(sem("eo_split"), done + EO_CREDIT)
                    for c in range(TT):
                        for part in (eo_hi, eo_lo):
                            nc.tensor.matmul(bank(c), selT[:, c * P:(c + 1) * P], part[:, :],
                                             start=False, stop=False, skip_group_check=True)

                gather(0)
                turn_gathered(0)

                def tile(e, t, change):
                    def layer1(q):
                        v = UNIT_OF[("1", q)]
                        pe.wait_ge(sem("wu_lo_done"), e * UNITS + v + 1)
                        cols = slice(q * 512, (q + 1) * 512)
                        nc.tensor.matmul(bank(4 + q % 2), ones_r[:, :], b1rows[:, cols], start=True, stop=False)
                        for k in range(KC):
                            wh, wl = wu_hi[:, v, k, :], wu_lo(v)[:, k, :]
                            nc.tensor.matmul(bank(4 + q % 2), gT_hi[:, k, :], wh, start=False, stop=False)
                            nc.tensor.matmul(bank(4 + q % 2), gT_hi[:, k, :], wl, start=False, stop=False)
                            ins = nc.tensor.matmul(bank(4 + q % 2), gT_lo[:, k, :], wh, start=False,
                                                   stop=(k == KC - 1))
                        ins.then_inc(sem("l1_made"), 1)

                    def turn_hidden(q):
                        pe.wait_ge(sem("h_made"), t * QT + q + 1)
                        if q == 0:
                            pe.wait_ge(sem("selT_done"), t + 1)
                        else:
                            pe.wait_ge(sem("h_lo"), t * QT + q)
                        for c in range(4):
                            ins = nc.tensor.matmul(bank(6)[:, c * P:(c + 1) * P], hid[:, q % 2, c * P:(c + 1) * P],
                                                   ident[:, :], is_transpose=True, start=True, stop=True)
                        ins.then_inc(sem("h_turned"), 1)

                    def layer2(q):
                        v = UNIT_OF[("2", q)]
                        pe.wait_ge(sem("wu_lo_done"), e * UNITS + v + 1)
                        pe.wait_ge(sem("h_lo"), t * QT + q + 1)
                        if q == 0:
                            pe.wait_ge(sem("gs_done"), t + 1)
                        for c in range(4):
                            first, last = q == 0 and c == 0, q == QT - 1 and c == 3
                            hh, hl = h_hi[:, q % 2, c, :], h_lo[:, q % 2, c, :]
                            wh, wl = wu_hi[:, v, c, :], wu_lo(v)[:, c, :]
                            nc.tensor.matmul(bank(7), hh, wh, start=first, stop=False)
                            nc.tensor.matmul(bank(7), hh, wl, start=False, stop=False)
                            ins = nc.tensor.matmul(bank(7), hl, wh, start=False, stop=last)
                        ins.then_inc(sem("l2_made"), 1)

                    pe.wait_ge(sem("g_lo"), t + 1)
                    pe.wait_ge(sem("b1row_in"), 16 * (e + 1))
                    layer1(0)
                    scatter(t)
                    for c in range(TT):
                        ins = nc.tensor.matmul(bank(6)[:, c * P:(c + 1) * P].bitcast(FR), sel[:, c, :], ident_r[:, :],
                                               is_transpose=True, start=True, stop=True)
                    ins.then_inc(sem("selT_made"), 1)
                    for c in range(TT):
                        ins = nc.tensor.matmul(bank(7)[:, 0:2], sel[:, c, :], gate2[:, c, :],
                                               start=(c == 0), stop=(c == TT - 1))
                    ins.then_inc(sem("gs_made"), 1)
                    layer1(1)
                    turn_hidden(0)
                    layer1(2)
                    turn_hidden(1)
                    layer2(0)
                    layer1(3)
                    turn_hidden(2)
                    layer2(1)
                    gather(t + 1)
                    turn_hidden(3)
                    layer2(2)
                    pe.wait_ge(sem("h_lo"), (t + 1) * QT)
                    turn_gathered(t + 1)
                    layer2(3)

                for_tiles(pe, tile)
                scatter(load_tile(pe, last_i, NE - 1) + 1)
                pe.drain().then_inc(sem("y_made"), 1)


_INS = ['x', 'ctx_1024', 'L0_xattn_Wq', 'L0_xattn_bq', 'L0_xattn_Wkv', 'L0_xattn_bkv', 'L0_xattn_Wproj',
        'L0_xattn_bproj', 'L0_attn_WQ', 'L0_attn_WK', 'L0_attn_WV_down', 'L0_attn_WV_up', 'L0_ffn_Wg', 'L0_ffn_bg',
        'L0_ffn_W1', 'L0_ffn_b1', 'L0_ffn_W2', 'L0_ffn_b2']
_OUTS = [((8, 64, 512), 'float32')]


def kernel(**inputs):
    import numpy as _np
    import concourse.bacc as _bacc
    from concourse import mybir as _mybir
    from concourse.bass_utils import run_bass_kernel_spmd as _run

    nc = _bacc.Bacc("TRN2", target_bir_lowering=False, num_devices=1)
    arrays, args = {}, []
    for name in _INS:
        a = _np.ascontiguousarray(inputs[name])
        arrays[f"in_{name}_dram"] = a
        args.append(nc.dram_tensor(f"in_{name}_dram", a.shape, _mybir.dt.from_np(a.dtype), kind="ExternalInput").ap())
    for i, (shape, dtype) in enumerate(_OUTS):
        dt = _mybir.dt.from_np(_np.dtype(dtype))
        args.append(nc.dram_tensor(f"out_{i}_dram", shape, dt, kind="ExternalOutput").ap())
    perceiver_kernel(nc, *args)
    r = _run(nc, [arrays], core_ids=[0])
    got = tuple(r.results[0][f"out_{i}_dram"] for i in range(len(_OUTS)))
    return got[0]
```
